# Optimizing a Trainium2 kernel written in Bass

```python
import numpy as np
import jax
import jax.numpy as jnp

def _softmax(x, axis=-1):
    return jax.nn.softmax(x, axis=axis)

def _gelu(x):
    return jax.nn.gelu(x, approximate=True)

def _silu(x):
    return jax.nn.silu(x)

def _sigmoid(x):
    return jax.nn.sigmoid(x)

def _layernorm(x, axis=-1, eps=1e-05):
    m = jnp.mean(x, axis=axis, keepdims=True)
    v = jnp.var(x, axis=axis, keepdims=True)
    return (x - m) / jnp.sqrt(v + eps)

def _scatter_add(tgt, idx, src, axis=0):
    return tgt.at[idx].add(src)

def _segment_sum(src, seg, n):
    return jax.ops.segment_sum(src, seg, n)
kernel_name = 'mk_seq_preln_d2_jaxref_r8_9810e1'

def setup_inputs(seed: int=0):
    np.random.seed(seed)
    _w = jnp.asarray

    def _L0_attn_setup():
        import jax, jax.numpy as jnp
        import numpy as np
        DIM, H, KV, HD, WIN = (128, 16, 4, 64, 64)
        EPS = 1e-06

        def rmsnorm(x, w, eps=EPS):
            return x * jax.lax.rsqrt(jnp.mean(x * x, axis=-1, keepdims=True) + eps) * w
        key = jax.random.key(seed)
        ks = jax.random.split(key, 7)
        B, T = (4, 256)
        s = 0.02
        return {'x': jax.random.normal(ks[0], (B, T, DIM), dtype=jnp.float32), 'wq': jax.random.normal(ks[1], (H * HD, DIM), dtype=jnp.float32) * s, 'wk': jax.random.normal(ks[2], (KV * HD, DIM), dtype=jnp.float32) * s, 'wv': jax.random.normal(ks[3], (KV * HD, DIM), dtype=jnp.float32) * s, 'wo': jax.random.normal(ks[4], (DIM, H * HD), dtype=jnp.float32) * s, 'q_norm_w': jnp.ones((HD,), dtype=jnp.float32), 'k_norm_w': jnp.ones((HD,), dtype=jnp.float32)}
    _L0_attn_in = _L0_attn_setup()

    def _L0_ffn_setup():
        import jax, jax.numpy as jnp
        import numpy as np
        B, S, D = (1, 256, 128)
        F = 176
        E = 16
        K = 2
        CAP_FACTOR = 1.25

        def _mlp(h, wg, wu, wd):
            return jax.nn.silu(h @ wg) * (h @ wu) @ wd
        key = jax.random.key(seed)
        ks = jax.random.split(key, 10)
        sd = 0.02
        return {'x': jax.random.normal(ks[0], (B, S, D), jnp.float32), 'router_w': jax.random.normal(ks[1], (D, E), jnp.float32) * sd, 'router_b': jnp.zeros((E,), jnp.float32), 'w_gate': jax.random.normal(ks[2], (E, D, F), jnp.float32) * sd, 'w_up': jax.random.normal(ks[3], (E, D, F), jnp.float32) * sd, 'w_down': jax.random.normal(ks[4], (E, F, D), jnp.float32) * sd, 'sw_gate': jax.random.normal(ks[5], (D, F), jnp.float32) * sd, 'sw_up': jax.random.normal(ks[6], (D, F), jnp.float32) * sd, 'sw_down': jax.random.normal(ks[7], (F, D), jnp.float32) * sd}
    _L0_ffn_in = _L0_ffn_setup()

    def _L1_attn_setup():
        import math
        import jax, jax.numpy as jnp
        import numpy as np
        DIM, NHEAD, TOPK = (128, 16, 64)
        DK = DIM // NHEAD
        HIDDEN = int(DIM * 8.0)
        EPS = 1e-05

        def _layernorm(x, g, b):
            mu = jnp.mean(x, axis=-1, keepdims=True)
            var = jnp.var(x, axis=-1, keepdims=True)
            return (x - mu) * jax.lax.rsqrt(var + EPS) * g + b

        def _adaptive_sparse_attn(xn, w_qkv, alpha_head, w_out):
            B, T, C = xn.shape
            qkv = xn @ w_qkv
            q, k, v = jnp.split(qkv, 3, axis=-1)

            def heads(t):
                return t.reshape(B, T, NHEAD, DK).transpose(0, 2, 1, 3)
            q, k, v = (heads(q), heads(k), heads(v))
            attn = jnp.einsum('bhqd,bhkd->bhqk', q, k) / math.sqrt(DK)
            dense = jnp.einsum('bhqk,bhkd->bhqd', jax.nn.softmax(attn, axis=-1), v)
            _, idx = jax.lax.top_k(attn, TOPK)
            M = B * NHEAD * T
            keep = jnp.zeros((M, T), bool).at[jnp.arange(M)[:, None], idx.reshape(M, TOPK)].set(True)
            keep = keep.reshape(B, NHEAD, T, T)
            attn_sp = jnp.where(keep, attn, jnp.float32(-1000000000.0))
            sparse = jnp.einsum('bhqk,bhkd->bhqd', jax.nn.softmax(attn_sp, axis=-1), v)
            gate = jax.nn.sigmoid(alpha_head)[None, :, None, None]
            out = gate * dense + (1.0 - gate) * sparse
            out = out.transpose(0, 2, 1, 3).reshape(B, T, C)
            return out @ w_out
        key = jax.random.key(seed)
        ks = jax.random.split(key, 12)
        B, T = (2, 256)
        s = 0.02
        return {'x': jax.random.normal(ks[0], (B, T, DIM), jnp.float32), 'ln1_g': jnp.ones((DIM,), jnp.float32), 'ln1_b': jnp.zeros((DIM,), jnp.float32), 'w_qkv': jax.random.normal(ks[1], (DIM, 3 * DIM), jnp.float32) * s, 'alpha_head': jnp.zeros((NHEAD,), jnp.float32), 'w_out': jax.random.normal(ks[2], (DIM, DIM), jnp.float32) * s, 'ln2_g': jnp.ones((DIM,), jnp.float32), 'ln2_b': jnp.zeros((DIM,), jnp.float32), 'w1': jax.random.normal(ks[3], (DIM, HIDDEN), jnp.float32) * s, 'b1': jnp.zeros((HIDDEN,), jnp.float32), 'w2': jax.random.normal(ks[4], (HIDDEN, DIM), jnp.float32) * s, 'b2': jnp.zeros((DIM,), jnp.float32), 'alpha': jnp.float32(0.5)}
    _L1_attn_in = _L1_attn_setup()

    def _L1_ffn_setup():
        import jax, jax.numpy as jnp
        import numpy as np
        MODEL_DIM = 128
        HIDDEN = 256
        NUM_GROUPS = 2
        EXPERTS_PER_GP = 4
        NUM_EXPERTS = NUM_GROUPS * EXPERTS_PER_GP
        TOP_K = 2
        B, T = (2, 256)

        def _swiglu(x):
            a, b = jnp.split(x, 2, axis=-1)
            return jax.nn.silu(a) * b
        key = jax.random.key(seed)
        ks = jax.random.split(key, 7)
        s = 0.02
        return {'x': jax.random.normal(ks[0], (B, T, MODEL_DIM), jnp.float32), 'w_in': jax.random.normal(ks[1], (HIDDEN * 2, MODEL_DIM), jnp.float32) * s, 'w_out': jax.random.normal(ks[2], (MODEL_DIM, HIDDEN), jnp.float32) * s, 'w1': jax.random.normal(ks[3], (HIDDEN * 2, MODEL_DIM), jnp.float32) * s, 'w2': jax.random.normal(ks[4], (NUM_EXPERTS, MODEL_DIM, HIDDEN), jnp.float32) * s, 'wg': jax.random.normal(ks[5], (NUM_GROUPS, MODEL_DIM), jnp.float32) * s, 'we': jax.random.normal(ks[6], (NUM_EXPERTS, MODEL_DIM), jnp.float32) * s, 'gb': jnp.zeros((NUM_GROUPS,), jnp.float32), 'eb': jnp.zeros((NUM_EXPERTS,), jnp.float32)}
    _L1_ffn_in = _L1_ffn_setup()
    _d = {'L0_attn_x': _L0_attn_in['x'], 'L0_attn_wq': _L0_attn_in['wq'], 'L0_attn_wk': _L0_attn_in['wk'], 'L0_attn_wv': _L0_attn_in['wv'], 'L0_attn_wo': _L0_attn_in['wo'], 'L0_attn_q_norm_w': _L0_attn_in['q_norm_w'], 'L0_attn_k_norm_w': _L0_attn_in['k_norm_w'], 'L0_ffn_router_w': _L0_ffn_in['router_w'], 'L0_ffn_router_b': _L0_ffn_in['router_b'], 'L0_ffn_w_gate': _L0_ffn_in['w_gate'], 'L0_ffn_w_up': _L0_ffn_in['w_up'], 'L0_ffn_w_down': _L0_ffn_in['w_down'], 'L0_ffn_sw_gate': _L0_ffn_in['sw_gate'], 'L0_ffn_sw_up': _L0_ffn_in['sw_up'], 'L0_ffn_sw_down': _L0_ffn_in['sw_down'], 'L1_attn_ln1_g': _L1_attn_in['ln1_g'], 'L1_attn_ln1_b': _L1_attn_in['ln1_b'], 'L1_attn_w_qkv': _L1_attn_in['w_qkv'], 'L1_attn_alpha_head': _L1_attn_in['alpha_head'], 'L1_attn_w_out': _L1_attn_in['w_out'], 'L1_attn_ln2_g': _L1_attn_in['ln2_g'], 'L1_attn_ln2_b': _L1_attn_in['ln2_b'], 'L1_attn_w1': _L1_attn_in['w1'], 'L1_attn_b1': _L1_attn_in['b1'], 'L1_attn_w2': _L1_attn_in['w2'], 'L1_attn_b2': _L1_attn_in['b2'], 'L1_attn_alpha': _L1_attn_in['alpha'], 'L1_ffn_w_in': _L1_ffn_in['w_in'], 'L1_ffn_w_out': _L1_ffn_in['w_out'], 'L1_ffn_w1': _L1_ffn_in['w1'], 'L1_ffn_w2': _L1_ffn_in['w2'], 'L1_ffn_wg': _L1_ffn_in['wg'], 'L1_ffn_we': _L1_ffn_in['we'], 'L1_ffn_gb': _L1_ffn_in['gb'], 'L1_ffn_eb': _L1_ffn_in['eb']}
    _x0 = _d['L0_attn_x']
    _d['L0_attn_x'] = jax.random.normal(jax.random.fold_in(jax.random.key(seed), 1), (1, 2048, 128), dtype=_x0.dtype)
    del _x0
    return _d

def reference(L0_attn_x, L0_attn_wq, L0_attn_wk, L0_attn_wv, L0_attn_wo, L0_attn_q_norm_w, L0_attn_k_norm_w, L0_ffn_router_w, L0_ffn_router_b, L0_ffn_w_gate, L0_ffn_w_up, L0_ffn_w_down, L0_ffn_sw_gate, L0_ffn_sw_up, L0_ffn_sw_down, L1_attn_ln1_g, L1_attn_ln1_b, L1_attn_w_qkv, L1_attn_alpha_head, L1_attn_w_out, L1_attn_ln2_g, L1_attn_ln2_b, L1_attn_w1, L1_attn_b1, L1_attn_w2, L1_attn_b2, L1_attn_alpha, L1_ffn_w_in, L1_ffn_w_out, L1_ffn_w1, L1_ffn_w2, L1_ffn_wg, L1_ffn_we, L1_ffn_gb, L1_ffn_eb):

    def _L0_attn_ref(x, wq, wk, wv, wo, q_norm_w, k_norm_w):
        import jax, jax.numpy as jnp
        import numpy as np
        DIM, H, KV, HD, WIN = (128, 16, 4, 64, 64)
        EPS = 1e-06

        def rmsnorm(x, w, eps=EPS):
            return x * jax.lax.rsqrt(jnp.mean(x * x, axis=-1, keepdims=True) + eps) * w
        B, T, D = x.shape
        rep = H // KV
        q = (x @ wq.T).reshape(B, T, H, HD)
        k = (x @ wk.T).reshape(B, T, KV, HD)
        v = (x @ wv.T).reshape(B, T, KV, HD)
        q = rmsnorm(q, q_norm_w)
        k = rmsnorm(k, k_norm_w)
        k = jnp.repeat(k, rep, axis=2)
        v = jnp.repeat(v, rep, axis=2)
        scores = jnp.einsum('bqhd,bkhd->bhqk', q, k) / jnp.sqrt(jnp.float32(HD))
        i = jnp.arange(T)[:, None]
        j = jnp.arange(T)[None, :]
        mask = (i >= j) & (i - j < WIN)
        scores = jnp.where(mask, scores, -jnp.inf)
        attn = jax.nn.softmax(scores, axis=-1)
        y = jnp.einsum('bhqk,bkhd->bqhd', attn, v).reshape(B, T, H * HD)
        return y @ wo.T

    def _L0_ffn_ref(x, router_w, router_b, w_gate, w_up, w_down, sw_gate, sw_up, sw_down):
        import jax, jax.numpy as jnp
        import numpy as np
        B, S, D = (1, 256, 128)
        F = 176
        E = 16
        K = 2
        CAP_FACTOR = 1.25

        def _mlp(h, wg, wu, wd):
            return jax.nn.silu(h @ wg) * (h @ wu) @ wd
        b, s, d = x.shape
        N = b * s
        NK = N * K
        C = int(np.ceil(CAP_FACTOR * NK / E))
        x_tokens = x.reshape(N, d)
        logits = x_tokens @ router_w + router_b
        probs = jax.nn.softmax(logits, axis=-1)
        vals, idx = jax.lax.top_k(probs, K)
        vals = vals / (jnp.sum(vals, axis=-1, keepdims=True) + 1e-09)
        idx_flat = idx.reshape(NK)
        vals_flat = vals.reshape(NK)
        oh_e = jax.nn.one_hot(idx_flat, E, dtype=x.dtype)
        pos = (jnp.cumsum(oh_e, axis=0) * oh_e).sum(axis=1) - 1
        within = (pos < C).astype(x.dtype)
        pos_c = jnp.clip(pos, 0, C - 1).astype(jnp.int32)
        token_ids = jnp.arange(NK) // K
        x_pair = x_tokens[token_ids] * within[:, None]
        expert_inputs = jnp.zeros((E, C, d), x.dtype).at[idx_flat, pos_c].add(x_pair)
        expert_outputs = jax.vmap(_mlp)(expert_inputs, w_gate, w_up, w_down)
        gathered = expert_outputs[idx_flat, pos_c] * (vals_flat * within)[:, None]
        output_tokens = gathered.reshape(N, K, d).sum(axis=1)
        return x + _mlp(x, sw_gate, sw_up, sw_down) + output_tokens.reshape(b, s, d)

    def _L1_attn_ref(x, ln1_g, ln1_b, w_qkv, alpha_head, w_out, ln2_g, ln2_b, w1, b1, w2, b2, alpha):
        import math
        import jax, jax.numpy as jnp
        import numpy as np
        DIM, NHEAD, TOPK = (128, 16, 64)
        DK = DIM // NHEAD
        HIDDEN = int(DIM * 8.0)
        EPS = 1e-05

        def _layernorm(x, g, b):
            mu = jnp.mean(x, axis=-1, keepdims=True)
            var = jnp.var(x, axis=-1, keepdims=True)
            return (x - mu) * jax.lax.rsqrt(var + EPS) * g + b

        def _adaptive_sparse_attn(xn, w_qkv, alpha_head, w_out):
            B, T, C = xn.shape
            qkv = xn @ w_qkv
            q, k, v = jnp.split(qkv, 3, axis=-1)

            def heads(t):
                return t.reshape(B, T, NHEAD, DK).transpose(0, 2, 1, 3)
            q, k, v = (heads(q), heads(k), heads(v))
            attn = jnp.einsum('bhqd,bhkd->bhqk', q, k) / math.sqrt(DK)
            dense = jnp.einsum('bhqk,bhkd->bhqd', jax.nn.softmax(attn, axis=-1), v)
            _, idx = jax.lax.top_k(attn, TOPK)
            M = B * NHEAD * T
            keep = jnp.zeros((M, T), bool).at[jnp.arange(M)[:, None], idx.reshape(M, TOPK)].set(True)
            keep = keep.reshape(B, NHEAD, T, T)
            attn_sp = jnp.where(keep, attn, jnp.float32(-1000000000.0))
            sparse = jnp.einsum('bhqk,bhkd->bhqd', jax.nn.softmax(attn_sp, axis=-1), v)
            gate = jax.nn.sigmoid(alpha_head)[None, :, None, None]
            out = gate * dense + (1.0 - gate) * sparse
            out = out.transpose(0, 2, 1, 3).reshape(B, T, C)
            return out @ w_out
        x = x + alpha * _adaptive_sparse_attn(_layernorm(x, ln1_g, ln1_b), w_qkv, alpha_head, w_out)
        h = jax.nn.gelu(_layernorm(x, ln2_g, ln2_b) @ w1 + b1, approximate=False)
        x = x + alpha * (h @ w2 + b2)
        return x

    def _L1_ffn_ref(x, w_in, w_out, w1, w2, wg, we, gb, eb):
        import jax, jax.numpy as jnp
        import numpy as np
        MODEL_DIM = 128
        HIDDEN = 256
        NUM_GROUPS = 2
        EXPERTS_PER_GP = 4
        NUM_EXPERTS = NUM_GROUPS * EXPERTS_PER_GP
        TOP_K = 2
        B, T = (2, 256)

        def _swiglu(x):
            a, b = jnp.split(x, 2, axis=-1)
            return jax.nn.silu(a) * b
        Bs, Ts, C = x.shape
        S = Bs * Ts
        flat = x.reshape(S, C)
        shared = _swiglu(flat @ w_in.T) @ w_out.T
        g_probs = jax.nn.softmax(flat @ wg.T + gb, axis=-1)
        g_idx = jnp.argmax(g_probs, axis=-1)
        e_logits = flat @ we.T + eb
        egid = jnp.arange(NUM_EXPERTS) // EXPERTS_PER_GP
        masked = jnp.where(g_idx[:, None] == egid[None, :], e_logits, -jnp.inf)
        e_probs = jax.nn.softmax(masked, axis=-1)
        g_prob = jnp.take_along_axis(g_probs, g_idx[:, None], axis=1)
        p_expert = e_probs * g_prob
        topv, topi = jax.lax.top_k(p_expert, TOP_K)
        w_se = jnp.zeros((S, NUM_EXPERTS), x.dtype).at[jnp.arange(S)[:, None], topi].add(topv)
        h = _swiglu(flat @ w1.T)
        routed = jnp.zeros_like(shared)
        for e in range(NUM_EXPERTS):
            routed = routed + h * w_se[:, e:e + 1] @ w2[e].T
        return (shared + routed).reshape(Bs, Ts, C)
    x = L0_attn_x
    x = x + _L0_attn_ref(_layernorm(x, axis=-1), L0_attn_wq, L0_attn_wk, L0_attn_wv, L0_attn_wo, L0_attn_q_norm_w, L0_attn_k_norm_w)
    x = x + _L0_ffn_ref(_layernorm(x, axis=-1), L0_ffn_router_w, L0_ffn_router_b, L0_ffn_w_gate, L0_ffn_w_up, L0_ffn_w_down, L0_ffn_sw_gate, L0_ffn_sw_up, L0_ffn_sw_down)
    x = x + _L1_attn_ref(_layernorm(x, axis=-1), L1_attn_ln1_g, L1_attn_ln1_b, L1_attn_w_qkv, L1_attn_alpha_head, L1_attn_w_out, L1_attn_ln2_g, L1_attn_ln2_b, L1_attn_w1, L1_attn_b1, L1_attn_w2, L1_attn_b2, L1_attn_alpha)
    x = x + _L1_ffn_ref(_layernorm(x, axis=-1), L1_ffn_w_in, L1_ffn_w_out, L1_ffn_w1, L1_ffn_w2, L1_ffn_wg, L1_ffn_we, L1_ffn_gb, L1_ffn_eb)
    return x

_drawn_inputs = setup_inputs


def setup_inputs(seed=0):
    import zlib

    import numpy as np

    out = dict(_drawn_inputs(seed))
    spreads = {'L0_attn_q_norm_w': (1.0, 0.6),
     'L0_attn_k_norm_w': (1.0, 0.6),
     'L0_ffn_router_b': (0.0, 0.8),
     'L1_attn_ln1_g': (1.0, 0.6),
     'L1_attn_ln1_b': (0.0, 0.8),
     'L1_attn_alpha_head': (0.0, 0.8),
     'L1_attn_ln2_g': (1.0, 0.6),
     'L1_attn_ln2_b': (0.0, 0.8),
     'L1_attn_b1': (0.0, 0.8),
     'L1_attn_b2': (0.0, 0.487),
     'L1_ffn_gb': (0.0, 0.8),
     'L1_ffn_eb': (0.0, 0.8)}
    factors = {'L0_ffn_router_w': 8.0,
     'L0_ffn_w_gate': 8.0,
     'L0_ffn_w_up': 8.0,
     'L0_ffn_w_down': 8.0,
     'L0_ffn_sw_gate': 8.0,
     'L0_ffn_sw_up': 8.0,
     'L0_ffn_sw_down': 8.0,
     'L1_attn_w_qkv': 8.0,
     'L1_attn_w_out': 8.0,
     'L1_attn_w1': 4.345,
     'L1_attn_w2': 3.87,
     'L1_ffn_w_in': 8.0,
     'L1_ffn_w_out': 8.0,
     'L1_ffn_w1': 8.0,
     'L1_ffn_w2': 8.0,
     'L1_ffn_wg': 8.0,
     'L1_ffn_we': 8.0}
    for name, (base, spread) in spreads.items():
        noise = np.random.default_rng([zlib.crc32(name.encode()), seed]).standard_normal(out[name].shape)
        drawn = base * np.exp(spread * noise) if base else spread * noise
        out[name] = jnp.asarray(drawn.astype(out[name].dtype))
    for name, factor in factors.items():
        out[name] = (out[name] * factor).astype(out[name].dtype)
    return out
```

```python
from contextlib import ExitStack

import numpy as np

import concourse.bass as bass
from concourse import mybir

F32 = mybir.dt.float32
BF16 = mybir.dt.bfloat16
I32 = mybir.dt.int32
ALU = mybir.AluOpType
ACT = mybir.ActivationFunctionType
AX_X = mybir.AxisListType.X
ds = bass.ds

P = 128
D = 128
T = 2048
NT = T // P
BLK = 512
NB = T // BLK
TPB = BLK // P
LN_EPS = 1e-5
NEG = -1e30

H0, KV0, HD0, WIN0 = 16, 4, 64, 64
RMS_EPS = 1e-6
SPAN = WIN0 + P
E0, F0, CAP0 = 16, 176, 320
F0R = F0 - P
F0W = 2 * P + 64 + F0R
H1, DK1, TOPK = 16, 8, 64
TERMS = 9
KROWS = TERMS * DK1
ROW_M, ROW_T = 96, 99
Z0 = 1.8627
HAZ = 0.889
WINDOW = 7
KBIG = 1e20
HID1 = 1024
E1, G1, HF1 = 8, 2, 256


class Sems:

    def __init__(self, nc):
        self.nc, self.held = nc, []

    def __call__(self, name):
        self.held.append(self.nc.alloc_semaphore(name=name))
        return self.held[-1]

    def renew(self):
        self.nc.all_engine_barrier()
        self.nc.clear_and_free_semaphores(self.held)
        self.nc.all_engine_barrier()
        self.held = []


def constants(nc, c, sem):
    ones_ready, picked = sem("const_ones"), sem("const_picked")
    with nc.Block() as block:
        @block.vector
        def _(dve):
            dve.memset(c["ident"][:], 1.0)
            dve.memset(c["sel8"][:], 1.0)
            dve.memset(c["strict"][:], 1.0)
            dve.memset(c["maskf"][:], 0.0)
            dve.memset(c["halfdiag"][:], 1.0)
            dve.memset(c["sumsel"][:], 1.0)
            dve.memset(c["powm"][:], -0.5).then_inc(ones_ready, 1)
            dve.wait_ge(picked, 1)
            dve.tensor_copy(c["identb"][:], c["ident"][:])
            dve.tensor_copy(c["maskb"][:, 0], c["maskf"][:, 0])
            dve.tensor_copy(c["maskb"][:, 1], c["maskf"][:, 1])
            dve.tensor_copy(c["strictb"][:], c["strict"][:])

        @block.gpsimd
        def _(pool):
            steps = [0]
            done = sem("const_step")

            def pick(t, pattern, base, mult, op, fill):
                if steps[0]:
                    pool.wait_ge(done, steps[0])
                pool.affine_select(out=t, in_=t, compare_op=op, fill=fill, base=base, pattern=pattern,
                                   channel_multiplier=mult).then_inc(done, 1)
                steps[0] += 1

            pool.wait_ge(ones_ready, 1)
            pick(c["ident"][:], [[-1, P]], 0, 1, ALU.is_equal, 0.0)
            pick(c["sel8"][:], [[-8, H1]], 0, 1, ALU.is_ge, 0.0)
            pick(c["sel8"][:], [[8, H1]], 7, -1, ALU.is_ge, 0.0)
            pick(c["strict"][:], [[1, P]], -1, -1, ALU.is_ge, 0.0)
            pick(c["halfdiag"][:, 0:64], [[0, 64]], 63, -1, ALU.is_ge, 0.0)
            pick(c["halfdiag"][:, 64:128], [[0, 64]], -64, 1, ALU.is_ge, 0.0)
            for k in range(2):
                v = c["sumsel"][:, k]
                pick(v[0:64], [[-1, 9]], -32 * k, 1, ALU.is_equal, 0.0)
                pick(v[64:128], [[-1, 9]], -32 * k, 1, ALU.is_equal, 0.0)
            for n in range(2):
                m = c["maskf"][:, n]
                pick(m, [[0, 2], [-1, SPAN]], WIN0, 1, ALU.is_ge, NEG)
                pick(m, [[0, 2], [1, SPAN]], -1, -1, ALU.is_ge, NEG)
            pick(c["maskf"][:, 0], [[0, 2], [1, SPAN]], -WIN0, 0, ALU.is_ge, NEG)
            pool.wait_ge(done, steps[0])
            pool.sem_inc(picked, 1)


def norm_tokens(nc, c, sem, tag, src, dst, dst_t, psum, gain=None, shift=None, load=None):
    mv_ready, rstd_ready = sem(tag + "mv"), sem(tag + "rstd")
    normed, turned, taken, st = sem(tag + "normed"), sem(tag + "turned"), sem(tag + "taken"), sem(tag + "st")
    loaded = sem(tag + "loaded")
    n_loads = len(load or [])
    with ExitStack() as ctx:
        stats = ctx.enter_context(nc.sbuf_tensor(tag + "stats", [P, NT, 6], F32))
        mv = ctx.enter_context(nc.sbuf_tensor(tag + "mvt", [P, NT, 2], F32))
        var = ctx.enter_context(nc.sbuf_tensor(tag + "var", [P, NT], F32))
        rstd = ctx.enter_context(nc.sbuf_tensor(tag + "rs", [P, NT], F32))
        block = ctx.enter_context(nc.Block())

        @block.sync
        def _(sp):
            for out, in_ in load or []:
                sp.dma_start(out, in_).then_inc(loaded, 16)
            if n_loads:
                sp.wait_ge(loaded, 16 * n_loads)

        @block.vector
        def _(dve):
            for i in range(NT):
                dve.bn_stats(stats[:, i], src[:, i]).then_inc(st, 1)
            for i in range(NT):
                dve.wait_ge(st, i + 1)
                dve.bn_aggr(mv[:, i], stats[:, i]).then_inc(st, 1)
            dve.wait_ge(st, 2 * NT)
            dve.tensor_scalar(var[:], mv[:, :, 1], LN_EPS, None, ALU.add).then_inc(mv_ready, 1)
            dve.wait_ge(rstd_ready, 1)
            for i in range(NT):
                dve.tensor_scalar(dst[:, i], src[:, i], mv[:, i, 0:1], rstd[:, i:i + 1],
                                  ALU.subtract, ALU.mult).then_inc(normed, 1)

        @block.gpsimd
        def _(pool):
            pool.wait_ge(mv_ready, 1)
            pool.tensor_tensor(rstd[:], var[:], c["powm"][:, 0:NT], ALU.pow).then_inc(rstd_ready, 1)

        @block.tensor
        def _(pe):
            for b in range(NB):
                if b >= 2:
                    pe.wait_ge(taken, b - 1)
                for j in range(TPB):
                    pe.wait_ge(normed, TPB * b + j + 1)
                    last = pe.transpose(psum[:, b % 2, j * P:(j + 1) * P], dst[:, TPB * b + j], c["ident"][:])
                last.then_inc(turned, 1)

        @block.scalar
        def _(act):
            if n_loads:
                act.wait_ge(loaded, 16 * n_loads)
            for b in range(NB):
                act.wait_ge(turned, b + 1)
                o = dst_t[:, b * BLK:(b + 1) * BLK]
                if gain is None:
                    act.copy(o, psum[:, b % 2]).then_inc(taken, 1)
                else:
                    act.activation(o, psum[:, b % 2], ACT.Identity, bias=shift, scale=gain).then_inc(taken, 1)


def window_project(nc, c, sem, ap, w, hn_t, ps):
    NC = 10
    loaded, wqk_ready = sem("p_loaded"), sem("p_wqk")
    ready, moved, squared, summed = sem("p_ready"), sem("p_moved"), sem("p_squared"), sem("p_summed")
    k_root, k_inv, q_root, q_inv = sem("p_kroot"), sem("p_kinv"), sem("p_qroot"), sem("p_qinv")
    v_ready, v_moved, padded = sem("p_vready"), sem("p_vmoved"), sem("p_padded")
    with ExitStack() as ctx:
        def sb(name, shape, dt=F32):
            return ctx.enter_context(nc.sbuf_tensor(name, shape, dt))

        wq, wkv = sb("p_wq", [P, H0 * HD0]), sb("p_wkv", [P, 2 * KV0 * HD0])
        qw, kw, qkw = sb("p_qw", [P, 1]), sb("p_kw", [P, 1]), sb("p_qkw", [P, 1])
        sq = [sb(f"p_sq{b}", [P, BLK]) for b in range(2)]
        q_rms, k_rms, k_scale = sb("p_qrms", [P, TPB * H0]), sb("p_krms", [P, BLK]), sb("p_ks", [P, BLK])
        rms_eps = sb("p_eps", [P, 1])
        block = ctx.enter_context(nc.Block())

        @block.sync
        def _(sp):
            sp.dma_start(wq[:], ap["wq"]).then_inc(loaded, 16)
            sp.dma_start(wkv[:], ap["wkv"]).then_inc(loaded, 16)
            for half in range(2):
                rows = slice(half * HD0, (half + 1) * HD0)
                sp.dma_start(qw[rows], ap["q_norm"]).then_inc(loaded, 16)
                sp.dma_start(kw[rows], ap["k_norm"]).then_inc(loaded, 16)

        @block.tensor
        def _(pe):
            pe.wait_ge(loaded, 16 * 6)

            def chunk(b, ch, first):
                n = b * NC + ch
                if not first:
                    pe.wait_ge(moved, n - 1)
                    pe.wait_ge(squared, n - 1)
                wt = wq[:, ch * P:(ch + 1) * P] if ch < 8 else wkv[:, (ch - 8) * P:(ch - 7) * P]
                pe.matmul(ps[:, ch % 2], wt, hn_t[:, ds(b * BLK, BLK)], start=True, stop=True).then_inc(ready, 1)

            def sums(b, ch):
                n = b * NC + ch
                pe.wait_ge(squared, n + 1)
                if ch < 8:
                    for j in range(TPB):
                        last = pe.matmul(ps[:, 2, j * H0 + 2 * ch:j * H0 + 2 * ch + 2], sq[ch % 2][:, j * P:(j + 1) * P],
                                         c["halfdiag"][:, 0:P:64], start=True, stop=True)
                else:
                    last = pe.matmul(ps[:, 3 + ch % 2], c["halfdiag"][:], sq[ch % 2][:], start=True, stop=True)
                last.then_inc(summed, 1)

            def blk(b, first):
                for ch in range(NC):
                    chunk(b, ch, first and ch < 2)
                    if ch == 0 and not first:
                        pe.wait_ge(q_root, b)
                        pe.wait_ge(k_root, 2 * b)
                    if ch:
                        sums(b, ch - 1)
                sums(b, NC - 1)

            blk(0, True)
            with pe.Fori(1, NB) as b:
                blk(b, False)
            for i in range(NT):
                if i >= 2:
                    pe.wait_ge(v_moved, i - 1)
                o = ps[:, 6 + i % 2]
                pe.matmul(o[:, 0:256], hn_t[:, i * P:(i + 1) * P], wkv[:, 256:512], start=True, stop=True)
                pe.matmul(o[0:WIN0, 256:512], hn_t[:, i * P + WIN0:(i + 1) * P], wkv[:, 256:512],
                          start=True, stop=True).then_inc(v_ready, 1)

        @block.scalar
        def _(act):
            def blk(b, first):
                for ch in range(NC):
                    n = b * NC + ch
                    act.wait_ge(ready, n + 1)
                    if not (first and ch < 2):
                        act.wait_ge(summed, n - 1)
                    act.activation(sq[ch % 2][:], ps[:, ch % 2], ACT.Square).then_inc(squared, 1)
                    if ch == 8:
                        act.wait_ge(summed, n)
                        if not first:
                            act.wait_ge(q_inv, b)
                        act.activation(q_rms[:], ps[:, 2, 0:TPB * H0], ACT.Sqrt, bias=rms_eps[:],
                                       scale=1.0 / HD0).then_inc(q_root, 1)
                    if ch >= 8:
                        act.wait_ge(summed, n + 1)
                        if not (first and ch == 8):
                            act.wait_ge(k_inv, 2 * b + ch - 8)
                        act.activation(k_rms[:], ps[:, 3 + ch % 2], ACT.Sqrt, bias=rms_eps[:],
                                       scale=1.0 / HD0).then_inc(k_root, 1)

            act.wait_ge(padded, 1)
            blk(0, True)
            with act.Fori(1, NB) as b:
                blk(b, False)
            for i in range(NT):
                act.wait_ge(v_ready, i + 1)
                act.copy(w["v"][:, i], ps[:, 6 + i % 2, 0:256])
                act.copy(w["v_old"][:, i + 1], ps[0:WIN0, 6 + i % 2, 256:512]).then_inc(v_moved, 1)

        @block.vector
        def _(dve):
            dve.memset(w["v_old"][:, 0], 0.0)
            dve.memset(w["k"][:, :, 0:WIN0], 0.0)
            dve.memset(rms_eps[:], RMS_EPS).then_inc(padded, 1)
            dve.wait_ge(loaded, 16 * 6)
            dve.scalar_tensor_tensor(out=qkw[:], in0=qw[:], scalar=HD0 ** -0.5, in1=kw[:], op0=ALU.mult,
                                     op1=ALU.mult).then_inc(wqk_ready, 1)
            dve.wait_ge(wqk_ready, 1)

            def blk(b, first):
                for ch in range(NC):
                    n = b * NC + ch
                    dve.wait_ge(squared, n + 1)
                    if ch < 8:
                        dve.tensor_copy(w["q"][:, ch, ds(b * BLK, BLK)], ps[:, ch % 2]).then_inc(moved, 1)
                        continue
                    if ch == 8:
                        dve.wait_ge(q_root, b + 1)
                        dve.reciprocal(w["rq"][:, ds(b * TPB * H0, TPB * H0)], q_rms[:]).then_inc(q_inv, 1)
                    dve.wait_ge(k_root, 2 * b + ch - 7)
                    if not (first and ch == 8):
                        dve.wait_ge(moved, n)
                    dve.reciprocal(k_scale[:], k_rms[:]).then_inc(k_inv, 1)
                    dve.wait_ge(k_inv, 2 * b + ch - 7)
                    dve.scalar_tensor_tensor(out=w["k"][:, ch - 8, ds(b * BLK + WIN0, BLK)], in0=ps[:, ch % 2],
                                             scalar=qkw[:], in1=k_scale[:], op0=ALU.mult,
                                             op1=ALU.mult).then_inc(moved, 1)

            blk(0, True)
            with dve.Fori(1, NB) as b:
                blk(b, False)


def window_attend(nc, c, sem, ap, w, x, ps):
    UN = 8
    loaded, staged = sem("w_loaded"), sem("w_staged")
    s_ready, m_ready, nb_ready, p_ready = sem("w_scores"), sem("w_max"), sem("w_nbias"), sem("w_probs")
    t_ready, tc_taken, to_taken = sem("w_turned"), sem("w_curtaken"), sem("w_oldtaken")
    pv_done, rd_ready, y_ready = sem("w_weighed"), sem("w_rden"), sem("w_y")
    yt_ready, yt_taken, out_ready, out_taken = sem("w_ytr"), sem("w_ytt"), sem("w_out"), sem("w_outtaken")
    with ExitStack() as ctx:
        def sb(name, shape, dt=F32):
            return ctx.enter_context(nc.sbuf_tensor(name, shape, dt))

        wo = sb("w_wo", [P, 8, D])
        q_t = [sb(f"w_q{b}", [P, 8, P]) for b in range(2)]
        k_t = [sb(f"w_k{b}", [P, 2, SPAN]) for b in range(2)]
        v_cur = [sb(f"w_vc{b}", [P, 256]) for b in range(2)]
        v_old = [sb(f"w_vo{b}", [WIN0, 256]) for b in range(2)]
        probs = [sb(f"w_p{b}", [P, 2, SPAN]) for b in range(2)]
        pt_cur = [sb(f"w_ptc{b}", [P, 2, P]) for b in range(2)]
        pt_old = [sb(f"w_pto{b}", [WIN0, 2, P]) for b in range(2)]
        top = [sb(f"w_top{b}", [P, 2]) for b in range(2)]
        nbias = [sb(f"w_nb{b}", [P, 2]) for b in range(2)]
        den = [sb(f"w_den{b}", [P, H0]) for b in range(2)]
        rden, y, y_t = sb("w_rd", [P, H0]), sb("w_yy", [P, H0, HD0]), sb("w_yyt", [P, 8, P])
        ps_s, ps_t, ps_y, ps_z, ps_o = ps[:, 0:3], ps[:, 3:5], ps[:, 5:7], ps[:, 7], ps[:, 7]
        S_BANK = [u % 3 for u in range(UN)]
        S_AGO = [2, 2, 5] + [3] * (UN - 3)
        block = ctx.enter_context(nc.Block())

        def slots(u):
            ch = 2 * (u // 2)
            return (2 * ch + u % 2, 2 * ch + 2 + u % 2)

        @block.sync
        def _(sp):
            sp.dma_start(wo[:], ap["wo"]).then_inc(loaded, 16)

        @block.gpsimd
        def _(pool):
            def stage(n, b):
                pool.tensor_copy(q_t[b][:], w["q"][:, :, ds(n * P, P)])
                pool.tensor_copy(k_t[b][:], w["k"][:, :, ds(n * P, SPAN)])
                pool.tensor_copy(v_cur[b][:], w["v"][:, ds(n, 1)].rearrange("p a d -> p (a d)"))
                pool.tensor_copy(v_old[b][:], w["v_old"][:, ds(n, 1)].rearrange("p a d -> p (a d)")).then_inc(staged, 1)

            stage(0, 0)
            stage(1, 1)
            with pool.Fori(1, NT // 2) as t:
                for b in range(2):
                    pool.wait_ge(pv_done, UN * (2 * t + b - 1))
                    pool.wait_ge(staged, 2)
                    stage(2 * t + b, b)

        @block.tensor
        def _(pe):
            def scores(k, u, b, early, first_tile):
                r = slice((u % 2) * HD0, (u % 2 + 1) * HD0)
                if not early:
                    pe.wait_ge(p_ready, k - S_AGO[u] + 1)
                o = ps_s[:, S_BANK[u]]
                pe.matmul(o[:, 0:2 * SPAN], c["identb"][:],
                          c["maskb"][:, 0 if first_tile else 1].rearrange("p a s -> p (a s)"),
                          start=True, stop=False, skip_group_check=True)
                for m, slot in enumerate(slots(u)):
                    ch = slot // 2
                    last = pe.matmul(o[:, m * SPAN:(m + 1) * SPAN], q_t[b][r, ch], k_t[b][r, ch // 4],
                                     start=False, stop=(m == 1), skip_group_check=True)
                last.then_inc(s_ready, 1)

            def turn(k, u, early):
                pe.wait_ge(p_ready, k + 1)
                if not early:
                    pe.wait_ge(tc_taken, k - 1)
                    pe.wait_ge(to_taken, k - 1)
                o = ps_t[:, u % 2].rearrange("p (m w q) -> p m w q", m=2, w=2)
                for m in range(2):
                    pe.transpose(o[:, m, 1], probs[u % 2][:, m, WIN0:SPAN], c["ident"][:])
                    last = pe.transpose(o[0:WIN0, m, 0], probs[u % 2][:, m, 0:WIN0], c["ident"][:])
                last.then_inc(t_ready, 1)

            def weigh(k, u, b):
                pe.wait_ge(tc_taken, k + 1)
                pe.wait_ge(to_taken, k + 1)
                for m, slot in enumerate(slots(u)):
                    kv = 2 * (slot // 8) + slot % 2
                    o = ps_y[:, slot // 8, (slot % 8) * HD0:(slot % 8 + 1) * HD0]
                    pe.matmul(o, pt_old[u % 2][:, m], v_old[b][:, kv * HD0:(kv + 1) * HD0], start=True, stop=False)
                    last = pe.matmul(o, pt_cur[u % 2][:, m], v_cur[b][:, kv * HD0:(kv + 1) * HD0],
                                     start=False, stop=True)
                last.then_inc(pv_done, 1)

            def turn_y(n, g):
                if g == 0:
                    pe.wait_ge(y_ready, n + 1)
                    if not (isinstance(n, int) and n == 0):
                        pe.wait_ge(out_taken, n)
                else:
                    pe.wait_ge(yt_taken, 2 * n + 1)
                for j in range(4):
                    s = 8 * g + 2 * j
                    last = pe.transpose(ps_z[:, j * P:(j + 1) * P],
                                        y[:, s:s + 2].rearrange("p a d -> p (a d)"), c["ident"][:])
                last.then_inc(yt_ready, 1)

            def project(n, chunks):
                if chunks[0] == 0:
                    pe.wait_ge(yt_taken, 2 * n + 2)
                for ch in chunks:
                    last = pe.matmul(ps_o[:, 0:D], y_t[:, ch], wo[:, ch], start=(ch == 0), stop=(ch == 7),
                                     skip_group_check=True)
                if chunks[-1] == 7:
                    last.then_inc(out_ready, 1)

            def output(n, u):
                if u in (2, 4):
                    turn_y(n, u // 2 - 1)
                elif u == 6:
                    project(n, range(4))
                elif u == 7:
                    project(n, range(4, 8))

            def pair(t, first, last):
                for b in range(2):
                    n = 2 * t + b
                    for u in range(UN):
                        k = UN * n + u
                        at_start = first and b == 0
                        if u + 2 < UN:
                            scores(k + 2, u + 2, b, at_start and u == 0, at_start)
                        elif not (last and b == 1):
                            if u + 2 == UN:
                                pe.wait_ge(staged, n + 2)
                            scores(k + 2, u + 2 - UN, 1 - b, False, False)
                        turn(k, u, at_start and u < 2)
                        if u:
                            if u == 1 and not at_start:
                                pe.wait_ge(y_ready, n)
                            weigh(k - 1, u - 1, b)
                        elif not at_start:
                            weigh(k - 1, UN - 1, 1 - b)
                        if not at_start:
                            output(n - 1, u)

            pe.wait_ge(loaded, 16)
            pe.wait_ge(staged, 1)
            scores(0, 0, 0, True, True)
            scores(1, 1, 0, True, True)
            pair(0, True, False)
            with pe.Fori(1, NT // 2 - 1) as t:
                pair(t, False, False)
            pair(NT // 2 - 1, False, True)
            weigh(UN * NT - 1, UN - 1, 1)
            for u in range(UN):
                output(NT - 1, u)

        @block.vector
        def _(dve):
            def take_cur(k, u):
                dve.wait_ge(t_ready, k + 1)
                if not (isinstance(k, int) and k < 2):
                    dve.wait_ge(pv_done, k - 1)
                dve.tensor_copy(pt_cur[u % 2][:], ps_t[:, u % 2].rearrange("p (m w q) -> p m w q", m=2, w=2)[:, :, 1]
                                ).then_inc(tc_taken, 1)

            def norm(n, b):
                dve.wait_ge(pv_done, UN * (n + 1))
                dve.reciprocal(rden[:], den[b][:]).then_inc(rd_ready, 1)
                dve.wait_ge(rd_ready, n + 1)
                if not (isinstance(n, int) and n == 0):
                    dve.wait_ge(yt_ready, 2 * n)
                for g in range(2):
                    last = dve.tensor_tensor(y[:, 8 * g:8 * g + 8], ps_y[:, g].rearrange("p (h d) -> p h d", h=8),
                                             rden[:, 8 * g:8 * g + 8].unsqueeze(2).to_broadcast([P, 8, HD0]), ALU.mult)
                last.then_inc(y_ready, 1)

            def add_out(n):
                dve.wait_ge(out_ready, n + 1)
                xn = x[:, ds(n, 1)].rearrange("p a d -> p (a d)") if not isinstance(n, int) else x[:, n]
                dve.tensor_tensor(xn, xn, ps_o[:, 0:D], ALU.add).then_inc(out_taken, 1)

            def pair(t, first):
                for b in range(2):
                    n = 2 * t + b
                    for u in range(UN):
                        k = UN * n + u
                        at_start = first and b == 0
                        dve.wait_ge(s_ready, k + 1)
                        if not (at_start and u < 2):
                            dve.wait_ge(nb_ready, k - 1)
                        dve.reduce_max(top[u % 2][:], ps_s[:, S_BANK[u], 0:2 * SPAN].rearrange("p (m s) -> p m s", m=2),
                                       AX_X).then_inc(m_ready, 1)
                        dve.wait_ge(m_ready, k + 1)
                        if not (at_start and u < 2):
                            dve.wait_ge(p_ready, k - 1)
                        dve.scalar_tensor_tensor(out=nbias[u % 2][:], in0=top[u % 2][:], scalar=-1.0,
                                                 in1=w["rq"][:, ds(n * H0 + slots(u)[0], 2, 2)],
                                                 op0=ALU.mult, op1=ALU.mult).then_inc(nb_ready, 1)
                        if not (at_start and u == 0):
                            take_cur(k - 1, (u - 1) % 2)
                        if u == 1 and not at_start:
                            norm(n - 1, 1 - b)
                        if u == 1 and not (at_start or first):
                            add_out(n - 2)

            pair(0, True)
            with dve.Fori(1, NT // 2) as t:
                pair(t, False)
            take_cur(UN * NT - 1, 1)
            norm(NT - 1, 1)
            add_out(NT - 2)
            add_out(NT - 1)

        @block.scalar
        def _(act):
            def take_old(k, u):
                act.wait_ge(tc_taken, k + 1)
                if not (isinstance(k, int) and k < 2):
                    act.wait_ge(pv_done, k - 1)
                act.copy(pt_old[u % 2][:], ps_t[0:WIN0, u % 2].rearrange("p (m w q) -> p m w q", m=2, w=2)[:, :, 0]
                         ).then_inc(to_taken, 1)

            def take_y(n, g):
                act.wait_ge(yt_ready, 2 * n + g + 1)
                act.copy(y_t[:, 4 * g:4 * g + 4].rearrange("p a q -> p (a q)"), ps_z).then_inc(yt_taken, 1)

            def pair(t, first):
                for b in range(2):
                    n = 2 * t + b
                    for u in range(UN):
                        k = UN * n + u
                        at_start = first and b == 0
                        act.wait_ge(nb_ready, k + 1)
                        if not (at_start and u < 2):
                            act.wait_ge(t_ready, k - 1)
                        if u == 0 and not first:
                            act.wait_ge(y_ready, n - 1)
                        for m, slot in enumerate(slots(u)):
                            last = act.activation(probs[u % 2][:, m], ps_s[:, S_BANK[u], m * SPAN:(m + 1) * SPAN], ACT.Exp,
                                                  bias=nbias[u % 2][:, m:m + 1], scale=w["rq"][:, ds(n * H0 + slot, 1)],
                                                  accum_out=den[b][:, slot:slot + 1])
                        last.then_inc(p_ready, 1)
                        if not (at_start and u == 0):
                            take_old(k - 1, (u - 1) % 2)
                        if u in (3, 5) and not at_start:
                            take_y(n - 1, u // 2 - 1)

            pair(0, True)
            with act.Fori(1, NT // 2) as t:
                pair(t, False)
            take_old(UN * NT - 1, 1)
            for g in range(2):
                take_y(NT - 1, g)


def route_top2(nc, c, sem, ap, hn_t, weight, ps):
    EN = E0
    loaded, scored = sem("r_loaded"), sem("r_scored")
    step, shifted, exped, masked, counted = sem("r_step"), sem("r_shift"), sem("r_exp"), sem("r_mask"), sem("r_count")
    with ExitStack() as ctx:
        def sb(name, shape, dt=F32):
            return ctx.enter_context(nc.sbuf_tensor(name, shape, dt))

        rw, rb = sb("r_w", [P, EN]), sb("r_b", [P, EN])
        logit, prob, mask = sb("r_l", [P, NT, EN]), sb("r_p", [P, NT, EN]), sb("r_m", [P, NT, EN])
        maskb, onesb = sb("r_mb", [P, NT, EN], BF16), sb("r_ones", [P, P], BF16)
        top8, total = sb("r_t8", [P, NT, 8]), sb("r_tot", [P, NT])
        picked, pair_sum = sb("r_pick", [P, NT, EN]), sb("r_ps", [P, NT])
        block = ctx.enter_context(nc.Block())

        @block.sync
        def _(sp):
            sp.dma_start(rw[:], ap["router_w"]).then_inc(loaded, 16)
            sp.dma_start(rb[:], ap["router_b"].to_broadcast([P, EN])).then_inc(loaded, 16)

        @block.tensor
        def _(pe):
            pe.wait_ge(loaded, 32)
            for i in range(NT):
                last = pe.matmul(ps[:, 0, i * EN:(i + 1) * EN], hn_t[:, i * P:(i + 1) * P], rw[:], start=True, stop=True)
            last.then_inc(scored, 1)
            pe.wait_ge(masked, 1)
            pe.matmul(ps[:, 1, 0:NT * EN], c["strictb"][:], maskb[:].rearrange("p i e -> p (i e)"),
                      start=True, stop=False, skip_group_check=True)
            for j in range(NT - 1):
                n = NT - 1 - j
                last = pe.matmul(ps[:, 1, (j + 1) * EN:NT * EN].rearrange("p (i e) -> p i e", e=EN), onesb[:],
                                 maskb[:, j:j + 1].to_broadcast([P, n, EN]), start=False, stop=(n == 1),
                                 skip_group_check=True)
            last.then_inc(counted, 1)

        @block.scalar
        def _(act):
            act.wait_ge(shifted, 1)
            act.activation(prob[:], prob[:], ACT.Exp).then_inc(exped, 1)

        @block.vector
        def _(dve):
            n = [0]

            def then(ins):
                n[0] += 1
                ins.then_inc(step, 1)
                dve.wait_ge(step, n[0])

            def spread(t):
                return t.unsqueeze(2).to_broadcast([P, NT, EN])

            dve.memset(onesb[:], 1.0)
            dve.wait_ge(loaded, 32)
            dve.wait_ge(scored, 1)
            then(dve.tensor_tensor(logit[:], ps[:, 0, 0:NT * EN].rearrange("p (i e) -> p i e", e=EN),
                                   rb[:].unsqueeze(1).to_broadcast([P, NT, EN]), ALU.add))
            for i in range(NT):
                last = dve.max(top8[:, i], logit[:, i])
            then(last)
            dve.tensor_tensor(maskb[:], logit[:], spread(top8[:, :, 1]), ALU.is_ge).then_inc(masked, 1)
            dve.tensor_tensor(prob[:], logit[:], spread(top8[:, :, 0]), ALU.subtract).then_inc(shifted, 1)
            dve.tensor_tensor(mask[:], logit[:], spread(top8[:, :, 1]), ALU.is_ge)
            dve.wait_ge(exped, 1)
            then(dve.reduce_sum(total[:], prob[:], AX_X))
            then(dve.reciprocal(total[:], total[:]))
            then(dve.tensor_tensor(prob[:], prob[:], spread(total[:]), ALU.mult))
            then(dve.tensor_tensor(picked[:], prob[:], mask[:], ALU.mult))
            then(dve.reduce_sum(pair_sum[:], picked[:], AX_X))
            then(dve.tensor_scalar(pair_sum[:], pair_sum[:], 1e-9, None, ALU.add))
            then(dve.reciprocal(pair_sum[:], pair_sum[:]))
            then(dve.tensor_tensor(picked[:], picked[:], spread(pair_sum[:]), ALU.mult))
            dve.wait_ge(counted, 1)
            dve.scalar_tensor_tensor(out=weight[:, :, 0:EN], in0=ps[:, 1, 0:NT * EN].rearrange("p (i e) -> p i e", e=EN),
                                     scalar=float(CAP0), in1=picked[:], op0=ALU.is_lt, op1=ALU.mult)
            dve.memset(weight[:, :, EN:EN + 1], 1.0)


def experts0(nc, c, sem, ap, x, hn, hn_t, weight, ps):
    loaded = [sem("e_loaded0"), sem("e_loaded1")]
    up_ready, silu_done, h_ready = sem("e_up"), sem("e_silu"), sem("e_h")
    down_ready, added, prev = sem("e_down"), sem("e_added"), sem("e_init")
    with ExitStack() as ctx:
        def sb(name, shape, dt=F32):
            return ctx.enter_context(nc.sbuf_tensor(name, shape, dt))

        wgu = [sb(f"e_gu{b}", [P, F0W]) for b in range(2)]
        wd0 = [sb(f"e_da{b}", [P, D]) for b in range(2)]
        wd1 = [sb(f"e_db{b}", [F0R, D]) for b in range(2)]
        s0 = [sb(f"e_s0{b}", [P, BLK]) for b in range(2)]
        s1 = [sb(f"e_s1{b}", [F0R, BLK]) for b in range(2)]
        h0 = [sb(f"e_h0{b}", [P, BLK]) for b in range(2)]
        h1 = [sb(f"e_h1{b}", [F0R, BLK]) for b in range(2)]
        block = ctx.enter_context(nc.Block())

        @block.sync
        def _(sp):
            def load(n, b, e):
                def at(t):
                    return t[e] if isinstance(e, int) else t[ds(e, 1)].rearrange("a p f -> (a p) f")
                sp.dma_start(wgu[b][:], at(ap["w_gu"])).then_inc(loaded[b], 16)
                sp.dma_start(wd0[b][:], at(ap["w_d0"])).then_inc(loaded[b], 16)
                sp.dma_start(wd1[b][:], at(ap["w_d1"])).then_inc(loaded[b], 16)

            load(0, 0, E0)
            load(1, 1, 0)
            sp.wait_ge(down_ready, NB)
            load(2, 0, 1)
            with sp.Fori(1, E0 // 2) as t:
                for b in (1, 0):
                    e = 2 * t + (1 - b)
                    sp.wait_ge(down_ready, NB * (e - 1) + NB)
                    load(e + 1, b, e)

        @block.tensor
        def _(pe):
            def up(k, b, j):
                o = ps[:, 3 * (j % 2):3 * (j % 2) + 3]
                r = hn_t[:, j * BLK:(j + 1) * BLK]
                pe.matmul(o[:, 0], wgu[b][:, 0:P], r, start=True, stop=True)
                pe.matmul(o[0:64 + F0R, 2], wgu[b][:, 2 * P:F0W], r, start=True, stop=True)
                pe.matmul(o[:, 1], wgu[b][:, P:2 * P], r, start=True, stop=True).then_inc(up_ready, 1)

            def down(k, b, j, early):
                pe.wait_ge(h_ready, k + 1)
                if not early:
                    pe.wait_ge(added, k - 1)
                for i in range(TPB):
                    o = ps[:, 6 + j % 2, i * D:(i + 1) * D]
                    pe.matmul(o, h0[j % 2][:, i * P:(i + 1) * P], wd0[b][:], start=True, stop=False)
                    last = pe.matmul(o, h1[j % 2][:, i * P:(i + 1) * P], wd1[b][:], start=False, stop=True)
                last.then_inc(down_ready, 1)

            def expert(n, b, first, last):
                for j in range(NB):
                    k = NB * n + j
                    if j + 1 < NB:
                        if not (first and j == 0):
                            pe.wait_ge(h_ready, k)
                        up(k + 1, b, j + 1)
                    elif not last:
                        pe.wait_ge(loaded[1 - b], 24 * (n + 2 + b))
                        pe.wait_ge(h_ready, k)
                        up(k + 1, 1 - b, 0)
                    down(k, b, j, first and j < 2)

            pe.wait_ge(loaded[0], 48)
            up(0, 0, 0)
            expert(0, 0, True, False)
            with pe.Fori(0, E0 // 2 - 1) as t:
                expert(2 * t + 1, 1, False, False)
                expert(2 * t + 2, 0, False, False)
            expert(E0 - 1, 1, False, False)
            expert(E0, 0, False, True)

        @block.scalar
        def _(act):
            def unit(k, j, early):
                act.wait_ge(up_ready, k + 1)
                if not early:
                    act.wait_ge(h_ready, k - 1)
                o = ps[:, 3 * (j % 2):3 * (j % 2) + 3]
                act.activation(s0[j % 2][:], o[:, 0], ACT.Silu)
                act.activation(s1[j % 2][:], o[0:F0R, 2], ACT.Silu).then_inc(silu_done, 1)

            for j in range(NB):
                unit(j, j, j < 2)
            with act.Fori(1, E0 + 1) as n:
                for j in range(NB):
                    unit(NB * n + j, j, False)

        @block.vector
        def _(dve):
            dve.tensor_tensor(x[:], x[:], hn[:], ALU.add).then_inc(prev, 1)

            def hidden(k, j, early):
                dve.wait_ge(silu_done, k + 1)
                if not early:
                    dve.wait_ge(down_ready, k - 1)
                o = ps[:, 3 * (j % 2):3 * (j % 2) + 3]
                dve.tensor_tensor(h1[j % 2][:], o[64:64 + F0R, 2], s1[j % 2][:], ALU.mult)
                dve.tensor_tensor(h0[j % 2][:], o[:, 1], s0[j % 2][:], ALU.mult).then_inc(h_ready, 1)

            def add(k, j, e, early):
                dve.wait_ge(down_ready, k + 1)
                if not early:
                    dve.wait_ge(added, k - 3)
                for i in range(TPB):
                    m = TPB * j + i
                    last = dve.scalar_tensor_tensor(out=x[:, m], in0=ps[:, 6 + j % 2, i * D:(i + 1) * D],
                                                    scalar=weight[:, m, ds(e, 1)], in1=x[:, m],
                                                    op0=ALU.mult, op1=ALU.add)
                last.then_inc(added, 1)

            dve.wait_ge(prev, 1)
            hidden(0, 0, True)
            for j in range(1, NB):
                hidden(j, j, j < 2)
                add(j - 1, j - 1, E0, True)
            hidden(NB, 0, False)
            add(NB - 1, NB - 1, E0, True)
            with dve.Fori(0, E0 - 1) as e:
                for j in range(NB):
                    k = NB * (e + 1) + j
                    hidden(k + 1, (j + 1) % NB, False)
                    add(k, j, e, False)
            for j in range(NB):
                k = NB * E0 + j
                if j + 1 < NB:
                    hidden(k + 1, j + 1, False)
                add(k, j, E0 - 1, False)


def attention_inputs(nc, c, sem, ap, y_t, v_all, nt0, sd0, parts, ps):
    loaded, projected, evacuated = sem("i_loaded"), sem("i_proj"), sem("i_evac")
    kv_ready, kv_taken, cov_ready, cov_taken = sem("i_kv"), sem("i_kvt"), sem("i_cov"), sem("i_covt")
    turned, multiplied, moment = sem("i_zq"), sem("i_r"), sem("i_mom")
    q_split, k_split, stored = sem("i_qs"), sem("i_ks"), sem("i_stored")
    ks = sem("i_kstep")
    step, var_ready, sd_ready = sem("i_step"), sem("i_var"), sem("i_sd")
    with ExitStack() as ctx:
        def sb(name, shape, dt=F32):
            return ctx.enter_context(nc.sbuf_tensor(name, shape, dt))

        w = sb("i_w", [P, 3 * D])
        q_t, k_t, prod = sb("i_q", [P, T]), sb("i_k", [P, T]), sb("i_prod", [P, T])
        k_tok = sb("i_ktok", [P, NT, D + 1])
        cov, k_sel = sb("i_cov_sb", [P, P]), sb("i_ksel", [P, H1])
        block8 = sb("i_b8", [P, P])
        var, mu2 = sb("i_var_sb", [P, H1 * NT]), sb("i_mu2", [P, H1 * NT])
        mean = sb("i_mean", [P, H1 * NT])
        qp = [sb(f"i_qp{n}", [P, T], BF16) for n in range(3)]
        kp = [sb(f"i_kp{n}", [P, T], BF16) for n in range(3)]
        q_res, k_res = sb("i_qres", [P, T]), sb("i_kres", [P, T])
        block = ctx.enter_context(nc.Block())

        @block.sync
        def _(sp):
            sp.dma_start(w[:], ap["w_qkv"]).then_inc(loaded, 16)
            for n in range(3):
                sp.wait_ge(q_split, n + 1)
                sp.dma_start(parts["q"][n], qp[n][:]).then_inc(stored, 16)
                sp.wait_ge(k_split, n + 1)
                sp.dma_start(parts["k"][n], kp[n][:]).then_inc(stored, 16)
            sp.wait_ge(stored, 96)

        @block.tensor
        def _(pe):
            pe.wait_ge(loaded, 16)
            for n in range(2):
                for b in range(NB):
                    pe.matmul(ps[:, 4 * n + b], w[:, n * D:(n + 1) * D], y_t[:, b * BLK:(b + 1) * BLK],
                              start=True, stop=True).then_inc(projected, 1)
            for i in range(NT):
                pe.wait_ge(evacuated, min(i, 7) + 1)
                if i >= 8:
                    pe.wait_ge(kv_taken, i - 7)
                pe.matmul(ps[:, i % 8, 0:2 * D], y_t[:, i * P:(i + 1) * P], w[:, D:3 * D],
                          start=True, stop=True).then_inc(kv_ready, 1)
            pe.wait_ge(kv_taken, NT)
            pe.wait_ge(step, 1)
            for i in range(NT):
                last = pe.matmul(ps[:, 0, 0:D + 1], k_tok[:, i, 0:D], k_tok[:, i], start=(i == 0), stop=(i == NT - 1))
            last.then_inc(cov_ready, 1)
            pe.wait_ge(cov_taken, 1)
            for b in range(NB):
                pe.matmul(ps[:, 1 + b], cov[:], q_t[:, b * BLK:(b + 1) * BLK], start=True, stop=True).then_inc(turned, 1)
            for i in range(NT):
                pe.wait_ge(multiplied, i // TPB + 1)
                pe.matmul(ps[:, 5, i * H1:(i + 1) * H1], q_t[:, i * P:(i + 1) * P], k_sel[:], start=True, stop=True)
                last = pe.matmul(ps[:, 6, i * H1:(i + 1) * H1], prod[:, i * P:(i + 1) * P], c["sel8"][:],
                                 start=True, stop=True)
            last.then_inc(moment, 1)

        @block.scalar
        def _(act):
            for b in range(NB):
                act.wait_ge(projected, b + 1)
                act.mul(q_t[:, b * BLK:(b + 1) * BLK], ps[:, b], DK1 ** -0.5).then_inc(evacuated, 1)
            for b in range(NB):
                act.wait_ge(projected, NB + b + 1)
                act.copy(k_t[:, b * BLK:(b + 1) * BLK], ps[:, 4 + b]).then_inc(evacuated, 1)
            for i in range(NT):
                act.wait_ge(kv_ready, i + 1)
                act.copy(k_tok[:, i, 0:D], ps[:, i % 8, 0:D])
                act.copy(v_all[:, i], ps[:, i % 8, D:2 * D]).then_inc(kv_taken, 1)
            act.wait_ge(var_ready, 1)
            act.activation(sd0[:], var[:], ACT.Sqrt).then_inc(sd_ready, 1)

        @block.vector
        def _(dve):
            n = [0]

            def then(ins):
                n[0] += 1
                ins.then_inc(step, 1)
                dve.wait_ge(step, n[0])

            dve.memset(k_tok[:, :, D:D + 1], 1.0)
            then(dve.tensor_copy(block8[:].rearrange("p (h e) -> p h e", e=DK1),
                                 c["sel8"][:].unsqueeze(2).to_broadcast([P, H1, DK1])))
            dve.wait_ge(evacuated, NB)
            dve.tensor_copy(qp[0][:], q_t[:]).then_inc(q_split, 1)
            dve.wait_ge(q_split, 1)
            then(dve.tensor_tensor(q_res[:], q_t[:], qp[0][:], ALU.subtract))
            dve.tensor_copy(qp[1][:], q_res[:]).then_inc(q_split, 1)
            dve.wait_ge(q_split, 2)
            then(dve.tensor_tensor(q_res[:], q_res[:], qp[1][:], ALU.subtract))
            dve.tensor_copy(qp[2][:], q_res[:]).then_inc(q_split, 1)
            dve.wait_ge(cov_ready, 1)
            dve.scalar_tensor_tensor(out=cov[:], in0=ps[:, 0, 0:D], scalar=1.0 / T, in1=block8[:],
                                     op0=ALU.mult, op1=ALU.mult)
            dve.scalar_tensor_tensor(out=k_sel[:], in0=ps[:, 0, D:D + 1].to_broadcast([P, H1]), scalar=1.0 / T,
                                     in1=c["sel8"][:], op0=ALU.mult, op1=ALU.mult).then_inc(cov_taken, 1)
            for b in range(NB):
                dve.wait_ge(turned, b + 1)
                dve.tensor_tensor(prod[:, b * BLK:(b + 1) * BLK], ps[:, 1 + b], q_t[:, b * BLK:(b + 1) * BLK],
                                  ALU.mult).then_inc(multiplied, 1)
            dve.wait_ge(moment, 1)
            then(dve.tensor_copy(mean[:].rearrange("p (h i) -> p i h", h=H1),
                                 ps[:, 5, 0:NT * H1].rearrange("p (i h) -> p i h", h=H1)))
            then(dve.tensor_tensor(mu2[:], mean[:], mean[:], ALU.mult))
            then(dve.tensor_tensor(var[:].rearrange("p (h i) -> p i h", h=H1),
                                   ps[:, 6, 0:NT * H1].rearrange("p (i h) -> p i h", h=H1),
                                   mu2[:].rearrange("p (h i) -> p i h", h=H1), ALU.subtract))
            dve.tensor_scalar(var[:], var[:], 1e-30, None, ALU.max).then_inc(var_ready, 1)
            dve.wait_ge(sd_ready, 1)
            dve.scalar_tensor_tensor(out=nt0[:], in0=sd0[:], scalar=-Z0, in1=mean[:], op0=ALU.mult, op1=ALU.subtract)

        @block.gpsimd
        def _(pool):
            pool.wait_ge(evacuated, 2 * NB)
            pool.tensor_scalar(kp[0][:], k_t[:], 0.0, 1.0, ALU.add, ALU.mult).then_inc(k_split, 1)
            pool.wait_ge(k_split, 1)
            pool.tensor_tensor(k_res[:], k_t[:], kp[0][:], ALU.subtract).then_inc(ks, 1)
            pool.wait_ge(ks, 1)
            pool.tensor_scalar(kp[1][:], k_res[:], 0.0, 1.0, ALU.add, ALU.mult).then_inc(k_split, 1)
            pool.wait_ge(k_split, 2)
            pool.tensor_tensor(k_t[:], k_res[:], kp[1][:], ALU.subtract).then_inc(ks, 1)
            pool.wait_ge(ks, 2)
            pool.tensor_scalar(kp[2][:], k_t[:], 0.0, 1.0, ALU.add, ALU.mult).then_inc(k_split, 1)


def find_thresholds(nc, c, sem, parts, stacks, nt0, sd0, thr, mx_all, ps):
    N2 = NT // 2
    loads = [sem(f"f_load{g}") for g in range(4)]
    q_cleared, k_cleared = sem("f_qcleared"), sem("f_kcleared")
    s_ready, act_done, dve_done, e_done = sem("f_scores"), sem("f_act"), sem("f_dve"), sem("f_near")
    updated, ranked, chain, imaged = sem("f_updated"), sem("f_ranked"), sem("f_chain"), sem("f_imaged")
    set_up, max_ready = sem("f_setup"), sem("f_max")
    with ExitStack() as ctx:
        def sb(name, shape, dt=F32):
            return ctx.enter_context(nc.sbuf_tensor(name, shape, dt))

        qs, ks = sb("f_q", [P, H1, T], BF16), sb("f_k", [P, H1, T], BF16)
        junk = [sb(f"f_junk{b}", [P, T], BF16) for b in range(2)]
        rej = [sb(f"f_rej{b}", [P, T]) for b in range(2)]
        near = sb("f_near_sb", [P, T])
        e_tmp = [sb(f"f_e{b}", [P, 8]) for b in range(2)]
        e8 = sb("f_e8", [P, NT, 8])
        acc, max_half = [sb(f"f_acc{s}", [P, NT, 2]) for s in range(3)], sb("f_maxhalf", [P, NT, 2])
        row_max = sb("f_rowmax", [P, NT])
        slot = {v: [None] + [sb(f"f_{v}{s}", [P, NT]) for s in range(1, 4)] for v in ("nt", "lo", "hi", "clo", "chi", "sd")}
        sgn, sgn_k, z0, dist = (sb(f"f_{n}", [P, NT]) for n in ("sgn", "sgnk", "z0", "dist"))
        bias_k = sb("f_biask", [P, NT, 2])
        tmp = {n: sb(f"f_t_{n}", [P, 8]) for n in ("c", "ge", "lt", "t", "a", "b", "d", "e", "nt", "sd", "lo", "f", "g")}
        wide = {n: sb(f"f_w_{n}", [P, 8, 8]) for n in ("zz", "x", "w", "v")}
        dist_all = sb("f_distall", [P, H1 * NT])
        rank8, minus1, pause = sb("f_rank", [P, 8]), sb("f_minus1", [P, 8]), sb("f_pause", [P, 1])
        search = ctx.enter_context(ExitStack())
        block = search.enter_context(nc.Block())

        ACT_OPS, DVE_OPS = (2, 2, 2, 2), (2, 0, 0, 2)
        HALF = T // 2
        plan = []
        before = [0, 0, 0]
        for v in range(H1 + 3):
            st = [s for s in range(4) if 0 <= v - s < H1]
            plan.append((st, *before))
            for k, ops in enumerate(((1, 1, 1, 1), ACT_OPS, DVE_OPS)):
                before[k] += NT * sum(ops[s] for s in st)
        FULL = 3

        def at(v):
            if isinstance(v, int):
                return plan[v][1:]
            return tuple(plan[FULL][1 + k] + NT * sum(ops) * (v - FULL)
                         for k, ops in enumerate(((1, 1, 1, 1), ACT_OPS, DVE_OPS)))

        def ops_of(steps, ops):
            return sum(ops[s] for s in steps)

        def half_row(p, h):
            return ps[:, 4 * (p % 2) + 2 * h:4 * (p % 2) + 2 * h + 2].rearrange("p a s -> p (a s)")

        def iterations(eng, run, peel=()):
            for v in range(FULL):
                run(v, plan[v][0])
            first = FULL
            while first in peel:
                run(first, plan[first][0])
                first += 1
            with eng.Fori(first, H1) as v:
                run(v, plan[FULL][0])
            for v in range(H1, H1 + 3):
                run(v, plan[v][0])

        @block.sync
        def _(sp):
            for g in range(4):
                for n in range(TERMS):
                    sp.wait_ge(q_cleared, g + 1)
                    sp.wait_ge(k_cleared, g + 1)
                    rows = slice(n * DK1, (n + 1) * DK1)
                    hs = slice(4 * g, 4 * g + 4)
                    for st, part in ((qs, parts["q"][n // 3]), (ks, parts["k"][n % 3])):
                        src = part.rearrange("(h d) t -> d h t", d=DK1)
                        sp.dma_start(st[rows, hs], src[:, hs]).then_inc(loads[g], 16)
            for g in range(4):
                sp.wait_ge(loads[g], 32 * TERMS)
                hs = slice(4 * g, 4 * g + 4)
                sp.dma_start(stacks["q"][hs].rearrange("h r t -> r h t"), qs[0:KROWS, hs]).then_inc(imaged, 16)
                sp.dma_start(stacks["k"][hs].rearrange("h r t -> r h t"), ks[0:KROWS, hs]).then_inc(imaged, 16)
            sp.wait_ge(imaged, 128)

        def wait_loads(eng, v):
            if isinstance(v, int) and v < H1:
                eng.wait_ge(loads[v // 4], 32 * TERMS)

        @block.tensor
        def _(pe):
            def run(v, steps):
                wait_loads(pe, v)
                if not isinstance(v, int):
                    for g in range(4):
                        pe.wait_ge(loads[g], 32 * TERMS)
                _, a0, d0 = at(v)
                local = [(o, s) for o in range(2) for s in steps]
                order = [s for _, s in local]
                na, nd = ops_of(order, ACT_OPS), ops_of(order, DVE_OPS)
                start = isinstance(v, int) and v == 0

                def left(ip, p, half):
                    done, base, per, ops = ((dve_done, d0, nd, DVE_OPS) if DVE_OPS[order[p - 2]] else
                                            (act_done, a0, na, ACT_OPS))
                    before_it = ops_of(order[:p - 2], ops) if p >= 2 else -ops_of(order[p - 2:], ops)
                    pe.wait_ge(done, base + ip * per + before_it + half + 1)

                def body(ip, early):
                    for p, (o, s) in enumerate(local):
                        h, i = v - s, 2 * ip + o
                        for half in range(2):
                            if not (early and p < 2):
                                left(ip, p, half)
                            for j in (2 * half, 2 * half + 1):
                                last = pe.matmul(ps[:, 4 * (p % 2) + j], qs[:, ds(h, 1), ds(i * P, P)].rearrange("p a q -> p (a q)"),
                                                 ks[:, ds(h, 1), j * BLK:(j + 1) * BLK].rearrange("p a q -> p (a q)"),
                                                 start=True, stop=True)
                            last.then_inc(s_ready, 1)

                if isinstance(v, int) and v and plan[v - 1][0][-2:] != steps[-2:]:
                    pe.wait_ge(act_done, a0)
                    pe.wait_ge(dve_done, d0)
                if start:
                    body(0, True)
                with pe.Fori(1 if start else 0, N2) as ip:
                    body(ip, False)

            iterations(pe, run, peel=(FULL,))

        @block.scalar
        def _(act):
            def run(v, steps):
                n0, a0, _ = at(v)
                n, na = 2 * len(steps), 2 * ops_of(steps, ACT_OPS)
                order = steps + steps

                def body(ip, early):
                    for p, s in enumerate(order):
                        o = p // len(steps)
                        i = 2 * ip + o
                        if s < 3 and not (early and p < 2):
                            act.wait_ge(act_done, a0 + ip * na + (ops_of(order[:p - 1], ACT_OPS) if p else -1))
                        if s < 3:
                            for h in range(2):
                                act.wait_ge(s_ready, 2 * (n0 + ip * n + p) + h + 1)
                                act.activation(junk[p % 2][:, h * HALF:(h + 1) * HALF], half_row(p, h), ACT.Sign,
                                               bias=slot["nt"][s][:, ds(i, 1)] if s else nt0[:, ds(v * NT + i, 1)],
                                               accum_out=acc[s][:, ds(i, 1), h]).then_inc(act_done, 1)
                        else:
                            for h in range(2):
                                act.wait_ge(s_ready, 2 * (n0 + ip * n + p) + h + 1)
                                act.activation(rej[o][:, h * HALF:(h + 1) * HALF], half_row(p, h), ACT.Relu,
                                               bias=bias_k[:, ds(i, 1), h], scale=sgn_k[:, ds(i, 1)]).then_inc(act_done, 1)

                for half in range(2):
                    start = isinstance(v, int) and v == 0 and half == 0
                    if not (isinstance(v, int) and v == 0):
                        act.wait_ge(updated, 2 * v + half - 1)
                    if start:
                        body(0, True)
                    with act.Fori(4 * half + start, 4 * half + 4) as ip:
                        body(ip, False)

            iterations(act, run)

        @block.vector
        def _(dve):
            for g in range(4):
                dve.memset(qs[64:P, 4 * g:4 * g + 4].rearrange("p h t -> p (h t)").bitcast(F32), 0.0).then_inc(q_cleared, 1)
            for j in range(8):
                dve.memset(rank8[:, j:j + 1], float(j))
            dve.memset(minus1[:], -1.0).then_inc(set_up, 1)

            def marked(at_near):
                dve.wait_ge(dve_done, at_near)
                dve.memset(pause[:], 0.0)

            def keep(f, col, o):
                dve.max(e_tmp[o][:], near[:]).then_inc(ranked, 1)
                dve.wait_ge(ranked, f + 1)
                out = e8[:, col] if isinstance(col, int) else e8[:, ds(col, 1)].rearrange("p a e -> p (a e)")
                dve.tensor_copy(out, e_tmp[o][:]).then_inc(e_done, 1)

            def run(v, steps):
                _, a0, d0 = at(v)
                na, nd = 2 * ops_of(steps, ACT_OPS), 2 * ops_of(steps, DVE_OPS)

                def body(ip, none_before):
                    for o in range(2):
                        i = 2 * ip + o
                        ranks = 3 in steps and not (none_before and o == 0)
                        acts = a0 + ip * na + o * na // 2
                        if ranks:
                            marked(d0 + ip * nd + o * nd // 2)
                        if 0 in steps:
                            for h in range(2):
                                dve.wait_ge(act_done, acts + h + 1)
                                dve.reduce_max(max_half[:, ds(i, 1), h], half_row(o * len(steps), h), AX_X
                                               ).then_inc(dve_done, 1)
                        if 3 in steps:
                            f = NT * (v - FULL) + i
                            if ranks:
                                col = NT - 1 if isinstance(ip, int) and ip == 0 and o == 0 else i - 1
                                keep(f - 1, col, 1 - o)
                        if 3 in steps:
                            for h in range(2):
                                dve.wait_ge(act_done, acts + na // 2 - 1 + h)
                                hs = slice(h * HALF, (h + 1) * HALF)
                                dve.scalar_tensor_tensor(out=near[:, hs], in0=half_row((o + 1) * len(steps) - 1, h),
                                                         scalar=sgn[:, ds(i, 1)], in1=rej[o][:, hs], op0=ALU.mult,
                                                         op1=ALU.subtract).then_inc(dve_done, 1)

                if not (0 in steps or 3 in steps):
                    return
                for half in range(2):
                    if not (isinstance(v, int) and v == 0):
                        dve.wait_ge(set_up, 1)
                        dve.wait_ge(updated, 2 * v + half - 1)
                    if half == 0:
                        body(0, isinstance(v, int) and v == FULL)
                    with dve.Fori(4 * half + (half == 0), 4 * half + 4) as ip:
                        body(ip, False)
                    if 0 in steps:
                        dve.wait_ge(dve_done, d0 + nd * (4 * half + 4))
                        cs = slice(8 * half, 8 * half + 8)
                        dve.tensor_tensor(row_max[:, cs], max_half[:, cs, 0], max_half[:, cs, 1], ALU.max
                                          ).then_inc(max_ready, 1)

            iterations(dve, run, peel=(FULL,))
            marked(plan[-1][3] + 2 * NT)
            keep(NT * H1 - 1, NT - 1, 1)

        @block.gpsimd
        def _(pool):
            for g in range(4):
                pool.memset(ks[64:P, 4 * g:4 * g + 4].rearrange("p h t -> p (h t)").bitcast(F32), 0.0).then_inc(k_cleared, 1)
            count = [0]

            def do(ins):
                ins.then_inc(chain, 1)
                count[0] += 1
                pool.wait_ge(chain, count[0])

            def tt(out, a, b, op):
                do(pool.tensor_tensor(out, a, b, op))

            def lin(out, a, mul, add):
                do(pool.tensor_scalar(out, a, mul, add, ALU.mult, ALU.add))

            def test(out, a, bound, op):
                do(pool.tensor_scalar(out, a, bound, 1.0, op, ALU.mult))

            def blend(out, g, a, l, b):
                tt(tmp["a"][:], g, a, ALU.mult)
                tt(tmp["b"][:], l, b, ALU.mult)
                tt(out, tmp["a"][:], tmp["b"][:], ALU.add)

            def update(v, s, half):
                cs = slice(8 * half, 8 * half + 8)
                h = v - s
                nxt = {k: slot[k][s + 1][:, cs] for k in slot}
                c_, ge, lt, t = (tmp[k][:] for k in ("c", "ge", "lt", "t"))
                if s == 0:
                    do(pool.tensor_copy(nxt["sd"], sd0[:, ds(h * NT + 8 * half, 8)]))
                    do(pool.tensor_copy(tmp["nt"][:], nt0[:, ds(h * NT + 8 * half, 8)]))
                    do(pool.tensor_copy(mx_all[:, ds(h * NT + 8 * half, 8)], row_max[:, cs]))
                    lin(t, tmp["nt"][:], -1.0, 0.0)
                    lin(tmp["a"][:], t, 1.1, 0.0)
                    lin(tmp["b"][:], nxt["sd"], -(1.1 * Z0 + 2.0), 0.0)
                    tt(tmp["a"][:], tmp["a"][:], tmp["b"][:], ALU.add)
                    lin(tmp["b"][:], row_max[:, cs], -0.1, 0.0)
                    tt(tmp["lo"][:], tmp["a"][:], tmp["b"][:], ALU.add)
                    tt(c_, acc[0][:, cs, 0], acc[0][:, cs, 1], ALU.add)
                    lin(c_, c_, 0.5, T / 2)
                    test(ge, c_, float(TOPK), ALU.is_ge)
                    lin(lt, ge, -1.0, 1.0)
                    blend(nxt["lo"], ge, t, lt, tmp["lo"][:])
                    blend(nxt["hi"], lt, t, ge, row_max[:, cs])
                    lin(tmp["d"][:], ge, 0.0, 1e4)
                    blend(nxt["clo"], ge, c_, lt, tmp["d"][:])
                    lin(tmp["d"][:], ge, 0.0, -1e4)
                    blend(nxt["chi"], lt, c_, ge, tmp["d"][:])
                else:
                    cur = {k: slot[k][s][:, cs] for k in slot}
                    lin(t, cur["nt"], -1.0, 0.0)
                    tt(c_, acc[s][:, cs, 0], acc[s][:, cs, 1], ALU.add)
                    lin(c_, c_, 0.5, T / 2)
                    test(ge, c_, float(TOPK), ALU.is_ge)
                    lin(lt, ge, -1.0, 1.0)
                    do(pool.tensor_copy(nxt["sd"], cur["sd"]))
                    blend(nxt["lo"], ge, t, lt, cur["lo"])
                    blend(nxt["hi"], lt, t, ge, cur["hi"])
                    blend(nxt["clo"], ge, c_, lt, cur["clo"])
                    blend(nxt["chi"], lt, c_, ge, cur["chi"])
                if s < 2:
                    d, e, f, g = (tmp[k][:] for k in ("d", "e", "f", "g"))
                    lin(d, c_, 1.0, float(TOPK))
                    tt(d, d, minus1[:], ALU.pow)
                    lin(e, c_, HAZ, -HAZ * TOPK)
                    tt(d, d, e, ALU.mult)
                    tt(d, d, nxt["sd"], ALU.mult)
                    tt(d, d, t, ALU.add)
                    tt(e, nxt["clo"], nxt["chi"], ALU.subtract)
                    tt(e, e, minus1[:], ALU.pow)
                    lin(f, nxt["clo"], 1.0, -float(TOPK))
                    tt(e, e, f, ALU.mult)
                    tt(f, nxt["hi"], nxt["lo"], ALU.subtract)
                    tt(e, e, f, ALU.mult)
                    tt(e, e, nxt["lo"], ALU.add)
                    test(f, nxt["clo"], 5000.0, ALU.is_lt)
                    test(g, nxt["chi"], -1.0, ALU.is_gt)
                    tt(f, f, g, ALU.mult)
                    lin(g, f, -1.0, 1.0)
                    blend(e, f, e, g, d)
                    lin(nxt["nt"], e, -1.0, 0.0)
                else:
                    best_side(cs, nxt)

            def best_side(cs, nxt):
                d, e, f, g = (tmp[k][:] for k in ("d", "e", "f", "g"))
                lin(d, nxt["clo"], 1.0, -float(TOPK))
                lin(e, nxt["chi"], -1.0, float(TOPK))
                tt(f, d, e, ALU.subtract)
                test(f, f, 0.0, ALU.is_gt)
                lin(g, f, -1.0, 1.0)
                blend(dist[:, cs], f, e, g, d)
                blend(e, f, nxt["hi"], g, nxt["lo"])
                lin(sgn[:, cs], f, 2.0, -1.0)
                tt(z0[:, cs], sgn[:, cs], e, ALU.mult)
                lin(sgn_k[:, cs], sgn[:, cs], KBIG, 0.0)
                lin(bias_k[:, cs], z0[:, cs].unsqueeze(2).to_broadcast([P, 8, 2]), -KBIG, 0.0)

            def settle(v, half):
                cs = slice(8 * half, 8 * half + 8)
                e, zz, x, w, u = e8[:, cs], wide["zz"], wide["x"][:], wide["w"][:], wide["v"][:]
                tt(zz[:, :, 1:8], e[:, :, 0:7], e[:, :, 1:8], ALU.add)
                tt(zz[:, :, 0], z0[:, cs], e[:, :, 0], ALU.add)
                tt(x, e, z0[:, cs].unsqueeze(2).to_broadcast([P, 8, 8]), ALU.subtract)
                test(w, x, 0.0, ALU.is_equal)
                tt(w[:, :, 0:4], w[:, :, 0:4], w[:, :, 4:8], ALU.add)
                tt(w[:, :, 0:2], w[:, :, 0:2], w[:, :, 2:4], ALU.add)
                tt(tmp["a"][:], w[:, :, 0], w[:, :, 1], ALU.add)
                lin(tmp["a"][:], tmp["a"][:], WINDOW + 1.0, 0.0)
                tt(dist[:, cs], dist[:, cs], tmp["a"][:], ALU.add)
                do(pool.tensor_copy(dist_all[:, ds((v - 3) * NT + 8 * half, 8)], dist[:, cs]))
                tt(x, rank8[:].unsqueeze(1).to_broadcast([P, 8, 8]), dist[:, cs].unsqueeze(2).to_broadcast([P, 8, 8]),
                   ALU.subtract)
                test(w, x, 0.0, ALU.is_ge)
                test(u, x, 1.0, ALU.is_lt)
                tt(w, w, u, ALU.mult)
                tt(zz[:], zz[:], w, ALU.mult)
                tt(zz[:, :, 0:4], zz[:, :, 0:4], zz[:, :, 4:8], ALU.add)
                tt(zz[:, :, 0:2], zz[:, :, 0:2], zz[:, :, 2:4], ALU.add)
                tt(tmp["a"][:], zz[:, :, 0], zz[:, :, 1], ALU.add)
                tt(tmp["a"][:], tmp["a"][:], sgn[:, cs], ALU.mult)
                lin(tmp["b"][:], tmp["a"][:], 0.5, 0.0)
                do(pool.tensor_copy(thr[:, ds((v - 3) * NT + 8 * half, 8)], tmp["b"][:]))

            def run(v, steps):
                _, a0, d0 = at(v)
                na, nd = ops_of(steps, ACT_OPS), ops_of(steps, DVE_OPS)
                pool.sem_clear(chain)
                count[0] = 0
                if isinstance(v, int) and v == 0:
                    pool.wait_ge(set_up, 1)
                    pool.wait_ge(k_cleared, 4)
                for half in range(2):
                    pool.wait_ge(act_done, a0 + 8 * na * (half + 1))
                    if nd:
                        pool.wait_ge(dve_done, d0 + 8 * nd * (half + 1))
                    if 0 in steps:
                        pool.wait_ge(max_ready, 2 * v + half + 1)
                    if 3 in steps:
                        pool.wait_ge(e_done, NT * (v - FULL) + 8 * (half + 1))
                        settle(v, half)
                    for s in (2, 1, 0):
                        if s in steps:
                            update(v, s, half)
                    pool.sem_inc(updated, 1)

            iterations(pool, run)

        search.close()
        rank_far_rows(nc, c, sem, qs, ks, dist_all, thr, near, ps)


def rank_far_rows(nc, c, sem, qs, ks, dist, thr, work, ps):
    far_ready, summed, flagged, numbered, scored, chosen, step = (sem("far_" + n) for n in (
        "found", "summed", "flagged", "numbered", "scored", "chosen", "step"))
    tiles = H1 * NT
    rounds = TOPK // 8
    with ExitStack() as ctx:
        def sb(name, shape, dt=F32):
            return ctx.enter_context(nc.sbuf_tensor("far_" + name, shape, dt))

        far, ones = sb("rows", [P, tiles]), sb("ones", [P, 1])
        number, left = sb("number", [1, tiles]), sb("left", [1, tiles])
        last8, total = sb("last8", [1, 8]), sb("total", [1, 1])
        how_many, tile, head = sb("how_many", [1, 1], I32), sb("tile", [1, 1], I32), sb("head", [1, 1], I32)
        top8 = [sb(f"top{r}", [P, 8]) for r in range(rounds + 1)]
        mid = sb("mid", [P, 1])
        block = ctx.enter_context(nc.Block())

        @block.gpsimd
        def _(pool):
            pool.iota(number[:], [[1, tiles]], base=1, channel_multiplier=0,
                      allow_small_or_imprecise_dtypes=True).then_inc(numbered, 1)

        @block.tensor
        def _(pe):
            pe.wait_ge(far_ready, 1)
            pe.matmul(ps[0:1, 0, 0:tiles], ones[:], far[:], start=True, stop=True).then_inc(summed, 1)
            pe.wait_ge(flagged, 1)
            n = pe.value_load(how_many[0:1, 0:1], min_val=0, max_val=tiles)
            with pe.Fori(0, n):
                pe.wait_ge(chosen, 1)
                pe.sem_clear(chosen)
                t = pe.value_load(tile[0:1, 0:1], min_val=0, max_val=tiles - 1)
                h = pe.value_load(head[0:1, 0:1], min_val=0, max_val=H1 - 1)
                for j in range(4):
                    last = pe.matmul(ps[:, 4 + j], qs[:].rearrange("p h t -> p (h t)")[:, ds(t * P, P)],
                                     ks[:, ds(h, 1), j * BLK:(j + 1) * BLK].rearrange("p a q -> p (a q)"),
                                     start=True, stop=True)
                last.then_inc(scored, 1)

        @block.vector
        def _(dve):
            steps = [0]

            def then(ins):
                steps[0] += 1
                ins.then_inc(step, 1)
                dve.wait_ge(step, steps[0])

            dve.memset(ones[:], 1.0)
            dve.tensor_scalar(far[:], dist[:], float(WINDOW), None, ALU.is_gt).then_inc(far_ready, 1)
            dve.wait_ge(numbered, 1)
            dve.wait_ge(summed, 1)
            then(dve.tensor_scalar(left[:], ps[0:1, 0, 0:tiles], 0.0, None, ALU.is_gt))
            then(dve.reduce_sum(total[:], left[:], AX_X))
            then(dve.tensor_tensor(left[:], left[:], number[:], ALU.mult))
            dve.tensor_copy(how_many[:], total[:]).then_inc(flagged, 1)
            dve.wait_ge(flagged, 1)
            n = dve.value_load(how_many[0:1, 0:1], min_val=0, max_val=tiles)
            with dve.Fori(0, n):
                dve.sem_clear(step)
                steps[0] = 0
                then(dve.max(last8[:], left[:]))
                then(dve.tensor_scalar(total[:], last8[:, 0:1], 1.0 / NT, -0.5 / NT - 0.5, ALU.mult, ALU.add))
                dve.tensor_copy(head[:], total[:])
                dve.tensor_scalar(tile[:], last8[:, 0:1], -1.0, None, ALU.add).then_inc(chosen, 1)
                then(dve.scalar_tensor_tensor(out=left[:], in0=left[:], scalar=last8[:, 0:1], in1=left[:],
                                              op0=ALU.is_lt, op1=ALU.mult))
                dve.wait_ge(scored, 1)
                dve.sem_clear(scored)
                t = dve.value_load(tile[0:1, 0:1], min_val=0, max_val=tiles - 1)
                then(dve.tensor_copy(work[:], ps[:, 4:8].rearrange("p a s -> p (a s)")))
                for r in range(rounds):
                    then(dve.max(top8[r][:], work[:]))
                    then(dve.match_replace(work[:], top8[r][:], work[:], NEG))
                then(dve.max(top8[rounds][:], work[:]))
                then(dve.tensor_tensor(mid[:], top8[rounds - 1][:, 7:8], top8[rounds][:, 0:1], ALU.add))
                then(dve.tensor_scalar(thr[:, ds(t, 1)], mid[:], 0.5, None, ALU.mult))


def shift_rows(nc, c, sem, thr, mx_all, shifts, ps):
    step, turned, taken, split, stored = sem("s_step"), sem("s_turn"), sem("s_taken"), sem("s_split"), sem("s_stored")
    with ExitStack() as ctx:
        def sb(name, shape, dt=F32):
            return ctx.enter_context(nc.sbuf_tensor(name, shape, dt))

        neg, res = sb("s_neg", [P, 4, P]), sb("s_res", [P, 4, P])
        part = [sb(f"s_p{n}", [P, 4, P], BF16) for n in range(3)]
        block = ctx.enter_context(nc.Block())

        @block.vector
        def _(dve):
            dve.tensor_tensor(thr[:], thr[:], mx_all[:], ALU.min).then_inc(step, 1)
            dve.wait_ge(taken, 1)
            dve.tensor_copy(part[0][:], neg[:]).then_inc(split, 1)
            dve.wait_ge(split, 1)
            dve.tensor_tensor(res[:], neg[:], part[0][:], ALU.subtract).then_inc(step, 1)
            dve.wait_ge(step, 2)
            dve.tensor_copy(part[1][:], res[:]).then_inc(split, 1)
            dve.wait_ge(split, 2)
            dve.tensor_tensor(neg[:], res[:], part[1][:], ALU.subtract).then_inc(step, 1)
            dve.wait_ge(step, 3)
            dve.tensor_copy(part[2][:], neg[:]).then_inc(split, 1)

        @block.tensor
        def _(pe):
            pe.wait_ge(step, 1)
            for n, src in enumerate((mx_all, thr)):
                for g in range(2):
                    last = pe.transpose(ps[:, 0, (2 * n + g) * P:(2 * n + g + 1) * P], src[:, g * P:(g + 1) * P],
                                        c["ident"][:])
            last.then_inc(turned, 1)

        @block.scalar
        def _(act):
            act.wait_ge(turned, 1)
            act.mul(neg[:], ps[:, 0].rearrange("p (a t) -> p a t", a=4), -1.0).then_inc(taken, 1)

        @block.sync
        def _(sp):
            for n in range(3):
                sp.wait_ge(split, n + 1)
                for k in range(2):
                    sp.dma_start(shifts[k][n].rearrange("(g p) t -> p g t", g=2), part[n][:, 2 * k:2 * k + 2]
                                 ).then_inc(stored, 16)
            sp.wait_ge(stored, 96)


def blend_heads(nc, c, sem, ap, stacks, shifts, v_all, o_all, ps):
    UN, QB = NT, NB
    LAG, KEPT = 3, 8
    loaded = [sem("b_loaded0"), sem("b_loaded1")]
    zeroed, ones, gate_in, gate_ready = sem("b_zeroed"), sem("b_ones"), sem("b_gatein"), sem("b_gate")
    v_ready, m_ready, t_ready = sem("b_v"), sem("b_m"), sem("b_t")
    exp_done, mask_done, pv_done = sem("b_exp"), sem("b_mask"), sem("b_pv")
    evac, summed, od_taken, fin = sem("b_evac"), sem("b_sum"), sem("b_od"), sem("b_fin")
    with ExitStack() as ctx:
        def sb(name, shape, dt=F32):
            return ctx.enter_context(nc.sbuf_tensor(name, shape, dt))

        k_m = [sb(f"b_km{b}", [P, T], BF16) for b in range(2)]
        k_th = [sb(f"b_kt{b}", [P, T], BF16) for b in range(2)]
        q = [sb(f"b_q{b}", [P, T], BF16) for b in range(2)]
        v9 = [sb(f"b_v9{b}", [P, NT, 32]) for b in range(2)]
        e = [sb(f"b_e{b}", [P, BLK]) for b in range(KEPT)]
        em = [sb(f"b_em{b}", [P, BLK]) for b in range(KEPT)]
        pv = sb("b_pvs", [P, BLK])
        od = sb("b_odt", [P, NT, 2, 9])
        rden, part = sb("b_rden", [P, NT, 2]), [sb(f"b_part{n}", [P, NT, DK1]) for n in range(2)]
        gate, gate_raw = sb("b_gates", [P, H1, 2]), sb("b_graw", [P, H1])
        block = ctx.enter_context(nc.Block())

        @block.sync
        def _(sp):
            sp.dma_start(gate_raw[:], ap["alpha_head"].to_broadcast([P, H1])).then_inc(gate_in, 16)
            sp.wait_ge(zeroed, 6)

            def load(h, b):
                def at(t):
                    return t[h] if isinstance(h, int) else t[ds(h, 1)].rearrange("a r t -> (a r) t")
                sp.dma_start(k_m[b][0:KROWS], at(stacks["k"])).then_inc(loaded[b], 16)
                sp.dma_start(q[b][0:KROWS], at(stacks["q"])).then_inc(loaded[b], 16)
                for row, s in ((ROW_M, shifts[0]), (ROW_T, shifts[1])):
                    src = s.rearrange("n (h i) t -> n h (i t)", h=H1)[:, ds(h, 1)].rearrange("n a t -> n (a t)")
                    sp.dma_start(q[b][row:row + 3], src).then_inc(loaded[b], 16)
                sp.dma_start(k_th[b][0:KROWS], at(stacks["k"])).then_inc(loaded[b], 16)

            load(0, 0)
            load(1, 1)
            with sp.Fori(1, H1 // 2) as t:
                for b in range(2):
                    sp.wait_ge(t_ready, UN * QB * (2 * t + b - 1))
                    load(2 * t + b, b)

        @block.gpsimd
        def _(pool):
            pool.wait_ge(ones, 1)

            def put(h, b):
                pool.tensor_copy(v9[b][:, :, 0:DK1], v_all[:, :, ds(h * DK1, DK1)]).then_inc(v_ready, 1)

            put(0, 0)
            put(1, 1)
            with pool.Fori(1, H1 // 2) as t:
                for b in range(2):
                    pool.wait_ge(pv_done, UN * QB * (2 * t + b - 1))
                    pool.wait_ge(ones, 1)
                    put(2 * t + b, b)

        @block.tensor
        def _(pe):
            def scores(k, b, qb, j, early):
                if not (early and j < 2):
                    pe.wait_ge(exp_done, k - 1)
                r = q[b][:, ds(qb * BLK, BLK)]
                pe.matmul(ps[:, j % 2], k_m[b][:, j * P:(j + 1) * P], r, start=True, stop=True).then_inc(m_ready, 1)
                if not (early and j < 4):
                    pe.wait_ge(mask_done, k - 3)
                pe.matmul(ps[:, 2 + j % 4], k_th[b][:, j * P:(j + 1) * P], r, start=True, stop=True).then_inc(t_ready, 1)

            def weigh(k, b, j):
                pe.wait_ge(exp_done, k + 1)
                g = 64 * (j % 2)
                pe.matmul(ps[g:g + 32, 6], v9[b][:, j], e[j % KEPT][:], start=(j < 2), stop=(j >= UN - 2))
                pe.wait_ge(mask_done, k + 1)
                pe.matmul(ps[g + 32:g + 64, 6], v9[b][:, j], em[j % KEPT][:], start=(j < 2), stop=(j >= UN - 2)
                          ).then_inc(pv_done, 1)

            def sums(g):
                pe.wait_ge(evac, g + 1)
                if not (isinstance(g, int) and g == 0):
                    pe.wait_ge(od_taken, g)
                for i in range(TPB):
                    last = pe.matmul(ps[:, 7, i * 18:(i + 1) * 18], pv[:, i * P:(i + 1) * P],
                                     c["sumsel"][:].rearrange("p a b -> p (a b)"), start=True, stop=True)
                last.then_inc(summed, 1)

            def group(h, qb, b, early, b_prev):
                g = QB * h + qb
                for j in range(UN):
                    k = UN * g + j
                    scores(k, b, qb, j, early)
                    if j < LAG:
                        if not early:
                            weigh(k - LAG, b_prev, UN - LAG + j)
                    elif j > LAG:
                        if j == LAG + 1:
                            if not early:
                                pe.wait_ge(evac, g)
                            weigh(k - LAG - 1, b, 0)
                        weigh(k - LAG, b, j - LAG)
                    if j == 6 and not early:
                        sums(g - 1)

            def head(h, b, first):
                if first:
                    pe.wait_ge(loaded[b], 80)
                    pe.wait_ge(v_ready, b + 1)
                else:
                    pe.wait_ge(loaded[b], 40 * (h + 2 - b))
                    pe.wait_ge(v_ready, h + 1)
                group(h, 0, b, first and b == 0, 1 - b)
                with pe.Fori(1, QB) as qb:
                    group(h, qb, b, False, b)

            head(0, 0, True)
            head(1, 1, True)
            with pe.Fori(1, H1 // 2) as t:
                head(2 * t, 0, False)
                head(2 * t + 1, 1, False)
            for j in range(UN - LAG, UN):
                weigh(UN * QB * H1 - UN + j, 1, j)
            sums(QB * H1 - 1)

        @block.scalar
        def _(act):
            act.wait_ge(gate_in, 16)
            act.activation(gate[:, :, 0], gate_raw[:], ACT.Sigmoid).then_inc(gate_ready, 1)

            def take(g):
                act.wait_ge(pv_done, UN * (g + 1))
                if not (isinstance(g, int) and g == 0):
                    act.wait_ge(summed, g)
                act.copy(pv[:], ps[:, 6]).then_inc(evac, 1)

            def group(g, early):
                for j in range(UN):
                    k = UN * g + j
                    act.wait_ge(m_ready, k + 1)
                    if not (early and j < KEPT):
                        act.wait_ge(pv_done, k - KEPT + 1)
                    act.activation(e[j % KEPT][:], ps[:, j % 2], ACT.Exp).then_inc(exp_done, 1)
                    if j == 2 and not early:
                        take(g - 1)

            group(0, True)
            with act.Fori(1, QB * H1) as g:
                group(g, False)
            take(QB * H1 - 1)

        @block.vector
        def _(dve):
            for t in k_m + k_th + q:
                dve.memset(t[64:P].bitcast(F32), 0.0).then_inc(zeroed, 1)
            dve.wait_ge(zeroed, 6)
            for b in range(2):
                dve.memset(k_m[b][96:99], 1.0)
                dve.memset(k_th[b][96:102], 1.0).then_inc(fin, 1)
            dve.wait_ge(fin, 2)
            for b in range(2):
                dve.memset(k_th[b][96:99], 0.0)
                dve.memset(v9[b][:], 0.0).then_inc(fin, 1)
            dve.wait_ge(fin, 4)
            dve.memset(v9[0][:, :, DK1:DK1 + 1], 1.0)
            dve.memset(v9[1][:, :, DK1:DK1 + 1], 1.0).then_inc(ones, 1)
            dve.wait_ge(gate_ready, 1)
            dve.tensor_scalar(gate[:, :, 1], gate[:, :, 0], -1.0, 1.0, ALU.mult, ALU.add).then_inc(fin, 1)
            F0 = 5

            def take_sums(g, qb):
                dve.wait_ge(summed, g + 1)
                dve.tensor_copy(od[:, ds(qb * TPB, TPB)].rearrange("p i a b -> p i (a b)"),
                                ps[:, 7, 0:TPB * 18].rearrange("p (i a) -> p i a", i=TPB)).then_inc(od_taken, 1)

            def finish(h, n):
                base = F0 + 4 * h
                if n == 0:
                    dve.wait_ge(od_taken, QB * (h + 1))
                    dve.reciprocal(rden[:], od[:, :, :, DK1]).then_inc(fin, 1)
                elif n == 1:
                    dve.wait_ge(fin, base + 1)
                    dve.tensor_tensor(rden[:], rden[:], gate[:, ds(h, 1)].to_broadcast([P, NT, 2]), ALU.mult).then_inc(fin, 1)
                elif n == 2:
                    dve.wait_ge(fin, base + 2)
                    for s in range(2):
                        last = dve.tensor_tensor(part[s][:], od[:, :, s, 0:DK1],
                                                 rden[:, :, s].unsqueeze(2).to_broadcast([P, NT, DK1]), ALU.mult)
                    last.then_inc(fin, 1)
                else:
                    dve.wait_ge(fin, base + 3)
                    dve.tensor_tensor(o_all[:, :, ds(h * DK1, DK1)], part[0][:], part[1][:], ALU.add).then_inc(fin, 1)

            def group(h, qb, early, head_start):
                g = QB * h + qb
                for j in range(UN):
                    k = UN * g + j
                    dve.wait_ge(exp_done, k + 1)
                    dve.wait_ge(t_ready, k + 1)
                    if not (early and j < KEPT):
                        dve.wait_ge(pv_done, k - KEPT + 1)
                    dve.scalar_tensor_tensor(out=em[j % KEPT][:], in0=ps[:, 2 + j % 4], scalar=0.0, in1=e[j % KEPT][:],
                                             op0=ALU.is_ge, op1=ALU.mult).then_inc(mask_done, 1)
                    if j == 8 and not early:
                        take_sums(g - 1, QB - 1 if head_start else qb - 1)
                    if head_start and not early and 9 <= j < 13:
                        finish(h - 1, j - 9)

            def head(h, early):
                group(h, 0, early, True)
                with dve.Fori(1, QB) as qb:
                    group(h, qb, False, False)

            head(0, True)
            with dve.Fori(1, H1) as h:
                head(h, False)
            take_sums(QB * H1 - 1, QB - 1)
            for n in range(4):
                finish(H1 - 1, n)


def project_heads(nc, c, sem, ap, o_all, y, ps):
    loaded, turned, taken, made = sem("j_loaded"), sem("j_turned"), sem("j_taken"), sem("j_made")
    with ExitStack() as ctx:
        def sb(name, shape, dt=F32):
            return ctx.enter_context(nc.sbuf_tensor(name, shape, dt))

        w, alpha, o_t = sb("j_w", [P, D]), sb("j_alpha", [P, 1]), sb("j_ot", [P, T])
        block = ctx.enter_context(nc.Block())

        @block.sync
        def _(sp):
            sp.dma_start(w[:], ap["w_out"]).then_inc(loaded, 16)
            sp.dma_start(alpha[:], ap["alpha"].to_broadcast([P, 1])).then_inc(loaded, 16)

        @block.tensor
        def _(pe):
            for b in range(NB):
                for j in range(TPB):
                    last = pe.transpose(ps[:, b, j * P:(j + 1) * P], o_all[:, TPB * b + j], c["ident"][:])
                last.then_inc(turned, 1)
            pe.wait_ge(loaded, 32)
            for b in range(NB):
                pe.wait_ge(taken, b + 1)
                for j in range(TPB):
                    i = TPB * b + j
                    last = pe.matmul(ps[:, 4 + b, j * P:(j + 1) * P], o_t[:, i * P:(i + 1) * P], w[:], start=True, stop=True)
                last.then_inc(made, 1)

        @block.scalar
        def _(act):
            for b in range(NB):
                act.wait_ge(turned, b + 1)
                act.copy(o_t[:, b * BLK:(b + 1) * BLK], ps[:, b]).then_inc(taken, 1)

        @block.vector
        def _(dve):
            dve.wait_ge(loaded, 32)
            for b in range(NB):
                dve.wait_ge(made, b + 1)
                yb = y[:, TPB * b:TPB * b + TPB].rearrange("p i d -> p (i d)")
                dve.scalar_tensor_tensor(out=yb, in0=ps[:, 4 + b], scalar=alpha[:], in1=yb, op0=ALU.mult, op1=ALU.add)


def mlp1(nc, c, sem, ap, x, y, z_t, ps):
    CH = HID1 // P
    loaded, up, hid, down, read, step = sem("m_loaded"), sem("m_up"), sem("m_hid"), sem("m_down"), sem("m_read"), sem("m_step")
    with ExitStack() as ctx:
        def sb(name, shape, dt=F32):
            return ctx.enter_context(nc.sbuf_tensor(name, shape, dt))

        w1, b1, w2 = sb("m_w1", [P, HID1]), sb("m_b1", [P, CH]), sb("m_w2", [P, CH, D])
        b2, alpha = sb("m_b2", [P, D]), sb("m_alpha", [P, 1])
        h = [sb(f"m_h{b}", [P, CH, BLK]) for b in range(2)]
        block = ctx.enter_context(nc.Block())

        @block.sync
        def _(sp):
            for out, in_ in ((w1, ap["w1"]), (b1, ap["b1"]), (w2, ap["w2"])):
                sp.dma_start(out[:], in_).then_inc(loaded, 16)
            sp.dma_start(b2[:], ap["b2"].to_broadcast([P, D])).then_inc(loaded, 16)
            sp.dma_start(alpha[:], ap["alpha"].to_broadcast([P, 1])).then_inc(loaded, 16)

        @block.tensor
        def _(pe):
            pe.wait_ge(loaded, 80)

            def ups(b):
                for ch in range(CH):
                    n = CH * b + ch
                    if n >= 4:
                        pe.wait_ge(hid, n - 3)
                    pe.matmul(ps[:, n % 4], w1[:, ch * P:(ch + 1) * P], z_t[:, b * BLK:(b + 1) * BLK],
                              start=True, stop=True).then_inc(up, 1)

            def downs(b):
                pe.wait_ge(hid, CH * (b + 1))
                if b >= 2:
                    pe.wait_ge(read, b - 1)
                for i in range(TPB):
                    for ch in range(CH):
                        last = pe.matmul(ps[:, 4 + b % 2, i * D:(i + 1) * D], h[b % 2][:, ch, i * P:(i + 1) * P], w2[:, ch],
                                         start=(ch == 0), stop=(ch == CH - 1))
                last.then_inc(down, 1)

            ups(0)
            for b in range(NB):
                if b + 1 < NB:
                    ups(b + 1)
                downs(b)

        @block.scalar
        def _(act):
            act.wait_ge(loaded, 80)
            for b in range(NB):
                if b >= 2:
                    act.wait_ge(down, b - 1)
                for ch in range(CH):
                    n = CH * b + ch
                    act.wait_ge(up, n + 1)
                    act.activation(h[b % 2][:, ch], ps[:, n % 4], ACT.Gelu, bias=b1[:, ch:ch + 1]).then_inc(hid, 1)

        @block.vector
        def _(dve):
            dve.wait_ge(loaded, 80)
            dve.tensor_scalar(b2[:], b2[:], alpha[:], None, ALU.mult)
            dve.tensor_tensor(x[:], x[:], y[:], ALU.add).then_inc(step, 1)
            dve.wait_ge(step, 1)
            dve.tensor_tensor(x[:], x[:], b2[:].unsqueeze(1).to_broadcast([P, NT, D]), ALU.add).then_inc(step, 1)
            dve.wait_ge(step, 2)
            for b in range(NB):
                dve.wait_ge(down, b + 1)
                xb = x[:, TPB * b:TPB * b + TPB].rearrange("p i d -> p (i d)")
                dve.scalar_tensor_tensor(out=xb, in0=ps[:, 4 + b % 2], scalar=alpha[:], in1=xb, op0=ALU.mult,
                                         op1=ALU.add).then_inc(read, 1)


def route_groups(nc, c, sem, ap, xn_t, weight, ps):
    EN = G1 + E1
    loaded, scored, step, shifted, exped = sem("g_loaded"), sem("g_scored"), sem("g_step"), sem("g_shift"), sem("g_exp")
    with ExitStack() as ctx:
        def sb(name, shape, dt=F32):
            return ctx.enter_context(nc.sbuf_tensor(name, shape, dt))

        rw, rb = sb("g_w", [P, EN]), sb("g_b", [P, EN])
        logit, high, low = sb("g_l", [P, NT, EN]), sb("g_high", [P, NT]), sb("g_low", [P, NT])
        first = sb("g_first", [P, NT, G1])
        masked, top8 = sb("g_masked", [P, NT, E1]), sb("g_top8", [P, NT, 8])
        ex = sb("g_ex", [P, NT, G1 + E1])
        total, mask = sb("g_total", [P, NT]), sb("g_mask", [P, NT, E1])
        block = ctx.enter_context(nc.Block())

        @block.sync
        def _(sp):
            sp.dma_start(rw[:], ap["w_route"]).then_inc(loaded, 16)
            sp.dma_start(rb[:], ap["b_route"].to_broadcast([P, EN])).then_inc(loaded, 16)

        @block.tensor
        def _(pe):
            pe.wait_ge(loaded, 32)
            for i in range(NT):
                last = pe.matmul(ps[:, 0, i * EN:(i + 1) * EN], xn_t[:, i * P:(i + 1) * P], rw[:], start=True, stop=True)
            last.then_inc(scored, 1)

        @block.scalar
        def _(act):
            act.wait_ge(shifted, 1)
            act.activation(ex[:], ex[:], ACT.Exp).then_inc(exped, 1)

        @block.vector
        def _(dve):
            n = [0]

            def then(ins):
                n[0] += 1
                ins.then_inc(step, 1)
                dve.wait_ge(step, n[0])

            def spread(t, m):
                return t.unsqueeze(2).to_broadcast([P, NT, m])

            dve.wait_ge(loaded, 32)
            dve.wait_ge(scored, 1)
            then(dve.tensor_tensor(logit[:], ps[:, 0, 0:NT * EN].rearrange("p (i e) -> p i e", e=EN),
                                   rb[:].unsqueeze(1).to_broadcast([P, NT, EN]), ALU.add))
            g0, g1 = logit[:, :, 0], logit[:, :, 1]
            then(dve.tensor_tensor(high[:], g0, g1, ALU.max))
            then(dve.tensor_tensor(first[:, :, 0], g0, g1, ALU.is_lt))
            then(dve.tensor_tensor(first[:, :, 1], g0, g1, ALU.is_ge))
            for g in range(G1):
                o = slice(4 * g, 4 * g + 4)
                last = dve.scalar_tensor_tensor(out=masked[:, :, o], in0=spread(first[:, :, g], 4), scalar=NEG,
                                                in1=logit[:, :, G1 + 4 * g:G1 + 4 * g + 4], op0=ALU.mult, op1=ALU.add)
            then(last)
            for i in range(NT):
                last = dve.max(top8[:, i], masked[:, i])
            then(last)
            dve.tensor_tensor(ex[:, :, 0:G1], logit[:, :, 0:G1], spread(high[:], G1), ALU.subtract)
            dve.tensor_tensor(ex[:, :, G1:EN], masked[:], spread(top8[:, :, 0], E1), ALU.subtract).then_inc(shifted, 1)
            dve.tensor_tensor(mask[:], masked[:], spread(top8[:, :, 1], E1), ALU.is_ge)
            dve.wait_ge(exped, 1)
            dve.reduce_sum(total[:], ex[:, :, 0:G1], AX_X)
            then(dve.reduce_sum(low[:], ex[:, :, G1:EN], AX_X))
            then(dve.tensor_tensor(total[:], total[:], low[:], ALU.mult))
            then(dve.reciprocal(total[:], total[:]))
            then(dve.tensor_tensor(mask[:], mask[:], ex[:, :, G1:EN], ALU.mult))
            dve.tensor_tensor(weight[:], mask[:], spread(total[:], E1), ALU.mult)


def experts1(nc, c, sem, ap, x, xn_t, weight, ps):
    loaded, up, silued, hid = sem("x_wloaded"), sem("x_up"), sem("x_silu"), sem("x_hid")
    down, read, chain = sem("x_down"), sem("x_read"), sem("x_chain")
    CH = HF1 // P
    with ExitStack() as ctx:
        def sb(name, shape, dt=F32):
            return ctx.enter_context(nc.sbuf_tensor(name, shape, dt))

        wi = sb("x_wi", [P, 2, 2 * HF1])
        wo, w2 = sb("x_wo", [P, CH, D]), sb("x_w2", [P, CH, E1 * D])
        sil = [sb(f"x_s{b}", [P, BLK]) for b in range(2)]
        h = [sb(f"x_h{b}", [P, 2, CH, BLK]) for b in range(2)]
        block = ctx.enter_context(nc.Block())

        @block.sync
        def _(sp):
            sp.dma_start(wi[:], ap["w_in"]).then_inc(loaded, 16)
            sp.dma_start(wo[:], ap["w_o"]).then_inc(loaded, 16)
            sp.dma_start(w2[:], ap["w_e"]).then_inc(loaded, 16)

        @block.tensor
        def _(pe):
            pe.wait_ge(loaded, 48)

            def ups(b):
                for u in range(4):
                    n = 4 * b + u
                    if n >= 2:
                        pe.wait_ge(hid, n - 1)
                    for part in range(2):
                        f = (u % 2) * P + part * HF1
                        last = pe.matmul(ps[:, 2 * (u % 2) + part], wi[:, u // 2, f:f + P], xn_t[:, b * BLK:(b + 1) * BLK],
                                         start=True, stop=True)
                    last.then_inc(up, 1)

            def downs(b):
                pe.wait_ge(hid, 4 * (b + 1))
                for i in range(TPB):
                    n = TPB * b + i
                    ts = slice(i * P, (i + 1) * P)
                    if n:
                        pe.wait_ge(read, 3 * n - 2)
                    for ch in range(CH):
                        last = pe.matmul(ps[:, 4, 0:D], h[b % 2][:, 0, ch, ts], wo[:, ch], start=(ch == 0), stop=(ch == CH - 1))
                    last.then_inc(down, 1)
                    for g in range(2):
                        if n:
                            pe.wait_ge(read, 3 * n - 1 + g)
                        for ch in range(CH):
                            last = pe.matmul(ps[:, 5 + g], h[b % 2][:, 1, ch, ts], w2[:, ch, g * BLK:(g + 1) * BLK],
                                             start=(ch == 0), stop=(ch == CH - 1))
                        last.then_inc(down, 1)

            ups(0)
            for b in range(NB):
                if b + 1 < NB:
                    ups(b + 1)
                downs(b)

        @block.scalar
        def _(act):
            for n in range(4 * NB):
                act.wait_ge(up, n + 1)
                if n >= 2:
                    act.wait_ge(hid, n - 1)
                act.activation(sil[n % 2][:], ps[:, 2 * (n % 2)], ACT.Silu).then_inc(silued, 1)

        @block.vector
        def _(dve):
            def hidden(b):
                for u in range(4):
                    n = 4 * b + u
                    dve.wait_ge(silued, n + 1)
                    if b >= 2 and u == 0:
                        dve.wait_ge(down, 3 * TPB * (b - 1))
                    dve.tensor_tensor(h[b % 2][:, u // 2, u % 2], ps[:, 2 * (u % 2) + 1], sil[n % 2][:], ALU.mult
                                      ).then_inc(hid, 1)

            def add(b):
                for i in range(TPB):
                    n = TPB * b + i
                    dve.wait_ge(down, 3 * n + 1)
                    dve.tensor_tensor(x[:, n], x[:, n], ps[:, 4, 0:D], ALU.add).then_inc(read, 1)
                    dve.wait_ge(read, 3 * n + 1)
                    for g in range(2):
                        dve.wait_ge(down, 3 * n + 2 + g)
                        for e in range(4):
                            k = 4 * g + e
                            ins = dve.scalar_tensor_tensor(out=x[:, n], in0=ps[:, 5 + g, e * D:(e + 1) * D],
                                                           scalar=weight[:, n, k:k + 1], in1=x[:, n],
                                                           op0=ALU.mult, op1=ALU.add)
                            if e < 3:
                                ins.then_inc(chain, 1)
                                dve.wait_ge(chain, 6 * n + 3 * g + e + 1)
                            else:
                                ins.then_inc(read, 1)
                                dve.wait_ge(read, 3 * n + 2 + g)

            hidden(0)
            for b in range(NB):
                if b + 1 < NB:
                    hidden(b + 1)
                add(b)




def program(nc, ap, out):
    with ExitStack() as ctx:
        def sb(name, shape, dt=F32):
            return ctx.enter_context(nc.sbuf_tensor(name, shape, dt))

        sem = Sems(nc)
        ps = ctx.enter_context(nc.psum_tensor("banks", [P, 8, BLK], F32))
        x = sb("x", [P, NT, D])
        c = {
            "ident": sb("ident", [P, P]), "identb": sb("identb", [P, P], BF16),
            "halfdiag": sb("halfdiag", [P, P]), "sel8": sb("sel8", [P, H1]),
            "strict": sb("strict", [P, P]), "strictb": sb("strictb", [P, P], BF16),
            "sumsel": sb("sumsel", [P, 2, 9]), "maskf": sb("maskf", [P, 2, 2, SPAN]),
            "maskb": sb("maskb", [P, 2, 2, SPAN], BF16),
            "powm": sb("powm", [P, NT]),
        }
        constants(nc, c, sem)
        with ExitStack() as layer:
            hn = layer.enter_context(nc.sbuf_tensor("hn", [P, NT, D], F32))
            hn_t = layer.enter_context(nc.sbuf_tensor("hn_t", [P, T], F32))
            load_tokens(nc, sem, x, ap["x"])
            norm_tokens(nc, c, sem, "n0", x, hn, hn_t, ps)
            with ExitStack() as att:
                w = {n: att.enter_context(nc.sbuf_tensor("w_all_" + n, s, F32)) for n, s in (
                    ("q", [P, 8, T]), ("k", [P, 2, WIN0 + T]), ("v", [P, NT, 256]), ("v_old", [WIN0, NT + 1, 256]),
                    ("rq", [P, NT * H0]))}
                window_project(nc, c, sem, ap, w, hn_t, ps)
                window_attend(nc, c, sem, ap, w, x, ps)
            norm_tokens(nc, c, sem, "n1", x, hn, hn_t, ps)
            weight = layer.enter_context(nc.sbuf_tensor("weight0", [P, NT, E0 + 1], F32))
            route_top2(nc, c, sem, ap, hn_t, weight, ps)
            experts0(nc, c, sem, ap, x, hn, hn_t, weight, ps)
        sem.renew()
        layer1(nc, c, sem, ap, x, ps)
        store_tokens(nc, sem, out, x)


def layer1(nc, c, sem, ap, x, ps):
    parts = {n: nc.dram_tensor("parts_" + n, [3, P, T], BF16).ap() for n in "qk"}
    stacks = {n: nc.dram_tensor("stacks_" + n, [H1, KROWS, T], BF16).ap() for n in "qk"}
    with ExitStack() as layer:
        def sb(name, shape, dt=F32):
            return layer.enter_context(nc.sbuf_tensor(name, shape, dt))

        y = sb("y", [P, NT, D])
        v_all = sb("v_all", [P, NT, D])
        nt0, sd0 = sb("nt0", [P, H1 * NT]), sb("sd0", [P, H1 * NT])
        thr, mx_all = sb("thr", [P, H1 * NT]), sb("mx_all", [P, H1 * NT])
        with ExitStack() as prep:
            yn = prep.enter_context(nc.sbuf_tensor("yn", [P, NT, D], F32))
            yn_t = prep.enter_context(nc.sbuf_tensor("yn_t", [P, T], F32))
            gb = prep.enter_context(nc.sbuf_tensor("ln1_gb", [P, 2], F32))
            norm_tokens(nc, c, sem, "n2", x, y, yn_t, ps)
            norm_tokens(nc, c, sem, "n3", y, yn, yn_t, ps, gain=gb[:, 0:1], shift=gb[:, 1:2],
                        load=[(gb[:, 0:1], ap["ln1_g"]), (gb[:, 1:2], ap["ln1_b"])])
            attention_inputs(nc, c, sem, ap, yn_t, v_all, nt0, sd0, parts, ps)
        find_thresholds(nc, c, sem, parts, stacks, nt0, sd0, thr, mx_all, ps)
        shifts = nc.dram_tensor("shifts", [2, 3, H1 * NT, P], BF16).ap()
        shift_rows(nc, c, sem, thr, mx_all, shifts, ps)
        o_all, z_t = sb("o_all", [P, NT, D]), sb("z_t", [P, T])
        blend_heads(nc, c, sem, ap, stacks, shifts, v_all, o_all, ps)
        project_heads(nc, c, sem, ap, o_all, y, ps)
        gb2 = sb("ln2_gb", [P, 2])
        norm_tokens(nc, c, sem, "n4", y, o_all, z_t, ps, gain=gb2[:, 0:1], shift=gb2[:, 1:2],
                    load=[(gb2[:, 0:1], ap["ln2_g"]), (gb2[:, 1:2], ap["ln2_b"])])
        mlp1(nc, c, sem, ap, x, y, z_t, ps)
        norm_tokens(nc, c, sem, "n5", x, o_all, z_t, ps)
        weight = sb("weight1", [P, NT, E1])
        route_groups(nc, c, sem, ap, z_t, weight, ps)
        experts1(nc, c, sem, ap, x, z_t, weight, ps)


def load_tokens(nc, sem, x, src):
    loaded = sem("x_loaded")
    with nc.Block() as block:
        @block.sync
        def _(sp):
            sp.dma_start(x[:], src.rearrange("(i p) d -> p i d", p=P)).then_inc(loaded, 16)
            sp.wait_ge(loaded, 16)


def store_tokens(nc, sem, out, x):
    stored = sem("x_stored")
    with nc.Block() as block:
        @block.sync
        def _(sp):
            sp.dma_start(out.rearrange("(i p) d -> p i d", p=P), x[:]).then_inc(stored, 16)
            sp.wait_ge(stored, 16)


def layouts(inputs):
    a = {k: np.asarray(v) for k, v in inputs.items()}
    L = {}
    L["x"] = a["L0_attn_x"].reshape(T, D)
    order = [4 * (2 * (ch // 4) + half) + ch % 4 for ch in range(8) for half in range(2)]
    wq = a["L0_attn_wq"].reshape(H0, HD0, D)[order].reshape(H0 * HD0, D)
    L["wq"] = wq.T
    L["wkv"] = np.concatenate([a["L0_attn_wk"], a["L0_attn_wv"]]).T
    wo = a["L0_attn_wo"].reshape(D, H0, HD0)[:, order].reshape(D, 8, P)
    L["wo"] = wo.transpose(2, 1, 0)
    L["q_norm"] = a["L0_attn_q_norm_w"].reshape(HD0, 1)
    L["k_norm"] = a["L0_attn_k_norm_w"].reshape(HD0, 1)
    L["router_w"], L["router_b"] = a["L0_ffn_router_w"], a["L0_ffn_router_b"].reshape(1, E0)
    gate = np.concatenate([a["L0_ffn_w_gate"], a["L0_ffn_sw_gate"][None]])
    up = np.concatenate([a["L0_ffn_w_up"], a["L0_ffn_sw_up"][None]])
    down = np.concatenate([a["L0_ffn_w_down"], a["L0_ffn_sw_down"][None]])
    pad = np.zeros((E0 + 1, D, 64 - F0R), np.float32)
    L["w_gu"] = np.concatenate([gate[:, :, :P], up[:, :, :P], gate[:, :, P:], pad, up[:, :, P:]], axis=2)
    L["w_d0"], L["w_d1"] = down[:, :P], down[:, P:]
    L["ln1_g"], L["ln1_b"] = a["L1_attn_ln1_g"].reshape(D, 1), a["L1_attn_ln1_b"].reshape(D, 1)
    L["w_qkv"] = a["L1_attn_w_qkv"]
    L["alpha_head"] = a["L1_attn_alpha_head"].reshape(1, H1)
    L["w_out"], L["alpha"] = a["L1_attn_w_out"], a["L1_attn_alpha"].reshape(1, 1)
    L["ln2_g"], L["ln2_b"] = a["L1_attn_ln2_g"].reshape(D, 1), a["L1_attn_ln2_b"].reshape(D, 1)
    L["w1"], L["b1"] = a["L1_attn_w1"], a["L1_attn_b1"].reshape(HID1 // P, P).T
    L["w2"] = a["L1_attn_w2"].reshape(HID1 // P, P, D).transpose(1, 0, 2)
    L["b2"] = a["L1_attn_b2"].reshape(1, D)
    L["w_route"] = np.concatenate([a["L1_ffn_wg"], a["L1_ffn_we"]]).T
    L["b_route"] = np.concatenate([a["L1_ffn_gb"], a["L1_ffn_eb"]]).reshape(1, G1 + E1)
    L["w_in"] = np.stack([a["L1_ffn_w_in"].T, a["L1_ffn_w1"].T], axis=1)
    L["w_o"] = a["L1_ffn_w_out"].T.reshape(HF1 // P, P, D).transpose(1, 0, 2)
    L["w_e"] = a["L1_ffn_w2"].transpose(2, 0, 1).reshape(HF1 // P, P, E1 * D).transpose(1, 0, 2)
    return {k: np.ascontiguousarray(v) for k, v in L.items()}


def kernel(**inputs):
    import concourse.bacc as bacc
    from concourse.bass_utils import run_bass_kernel_spmd

    arrays = layouts(inputs)
    nc = bacc.Bacc("TRN2", target_bir_lowering=False, num_devices=1)
    ap = {k: nc.dram_tensor("in_" + k, v.shape, mybir.dt.from_np(v.dtype), kind="ExternalInput").ap()
          for k, v in arrays.items()}
    out = nc.dram_tensor("out_x", (T, D), F32, kind="ExternalOutput").ap()
    program(nc, ap, out)
    r = run_bass_kernel_spmd(nc, [{"in_" + k: v for k, v in arrays.items()}], core_ids=[0])
    return r.results[0]["out_x"].reshape(1, T, D)
```
